# Optimizing a Trainium2 kernel written in Bass

```python
import numpy as np
import jax
import jax.numpy as jnp

def _softmax(x, axis=-1):
    return jax.nn.softmax(x, axis=axis)

def _gelu(x):
    return jax.nn.gelu(x, approximate=True)

def _silu(x):
    return jax.nn.silu(x)

def _sigmoid(x):
    return jax.nn.sigmoid(x)

def _layernorm(x, axis=-1, eps=1e-05):
    m = jnp.mean(x, axis=axis, keepdims=True)
    v = jnp.var(x, axis=axis, keepdims=True)
    return (x - m) / jnp.sqrt(v + eps)

def _scatter_add(tgt, idx, src, axis=0):
    return tgt.at[idx].add(src)

def _segment_sum(src, seg, n):
    return jax.ops.segment_sum(src, seg, n)
kernel_name = 'mk_cond_seq_d2_seqx_r4_335717'

def setup_inputs(seed: int=0):
    np.random.seed(seed)
    _w = jnp.asarray

    def _rec_inputs():
        import jax
        import jax.numpy as jnp
        _rk = jax.random.key(seed)
        x = 7.22e-05 + 1 * jax.random.normal(jax.random.fold_in(_rk, 1), (4, 512, 256), jnp.float32)
        _lenS = 512 - jax.random.randint(jax.random.fold_in(_rk, 7), (4,), 0, max(1, 512 // 4) + 1, jnp.int32)
        _lenS2 = 512 - jax.random.randint(jax.random.fold_in(_rk, 8), (4,), 0, max(1, 512 // 4) + 1, jnp.int32)
        cond_2048 = 0.00782532 + 1.00527 * jax.random.normal(jax.random.fold_in(_rk, 11), (4, 512), jnp.float32)
        _validS = jnp.arange(512)[None, :] < _lenS[:, None]
        _validS2 = jnp.arange(512)[None, :] < _lenS2[:, None]
        _causal = jnp.tril(jnp.ones((512, 512), dtype=bool))
        mask_BxSx1_fk1 = jnp.where(jnp.ones((4, 512, 1), dtype=bool), 1.0, 0.0).astype(jnp.float32)
        mask_BxS_ff1 = jnp.where(jnp.ones((4, 512), dtype=bool), 1.0, 0.0).astype(jnp.float32)
        return (x, cond_2048, mask_BxSx1_fk1, mask_BxS_ff1)
    x, cond_2048, mask_BxSx1_fk1, mask_BxS_ff1 = _rec_inputs()

    def _L0_cond_setup():
        import jax, jax.numpy as jnp
        import numpy as np
        B, T, D, H, TE = (4, 512, 256, 8, 512)
        EPS = 1e-05

        def _ln(x, w, b):
            m = jnp.mean(x, axis=-1, keepdims=True)
            v = jnp.mean((x - m) ** 2, axis=-1, keepdims=True)
            return (x - m) * jax.lax.rsqrt(v + EPS) * w + b
        key = jax.random.key(seed)
        ks = jax.random.split(key, 16)
        s = 0.02
        inp = {'x': jax.random.normal(ks[0], (B, T, D), jnp.float32), 'emb': jax.random.normal(ks[1], (B, TE), jnp.float32), 'src_mask': (jax.random.uniform(ks[2], (B, T, 1)) > 0.2).astype(jnp.float32), 'num_head': H, 'ln_w': jnp.ones((D,), jnp.float32), 'ln_b': jnp.zeros((D,), jnp.float32), 'Wq': jax.random.normal(ks[3], (D, D), jnp.float32) * s, 'bq': jnp.zeros((D,), jnp.float32), 'Wk': jax.random.normal(ks[4], (D, D), jnp.float32) * s, 'bk': jnp.zeros((D,), jnp.float32), 'Wv': jax.random.normal(ks[5], (D, D), jnp.float32) * s, 'bv': jnp.zeros((D,), jnp.float32), 'W_emb': jax.random.normal(ks[6], (TE, 2 * D), jnp.float32) * s, 'b_emb': jnp.zeros((2 * D,), jnp.float32), 'ln2_w': jnp.ones((D,), jnp.float32), 'ln2_b': jnp.zeros((D,), jnp.float32), 'W_out': jax.random.normal(ks[7], (D, D), jnp.float32) * s, 'b_out': jnp.zeros((D,), jnp.float32)}
        return inp
    _L0_cond_all = _L0_cond_setup()
    _L0_cond_in = {k: v for k, v in _L0_cond_all.items() if k in ('ln_w', 'ln_b', 'Wq', 'bq', 'Wk', 'bk', 'Wv', 'bv', 'W_emb', 'b_emb', 'ln2_w', 'ln2_b', 'W_out', 'b_out')}
    del _L0_cond_all

    def _L1_cond_setup():
        import jax, jax.numpy as jnp
        import numpy as np
        B, T, D, H, TE = (8, 256, 256, 16, 512)
        LN_EPS = 1e-05

        def layer_norm(x, w, b):
            m = jnp.mean(x, axis=-1, keepdims=True)
            v = jnp.var(x, axis=-1, keepdims=True)
            return (x - m) / jnp.sqrt(v + LN_EPS) * w + b
        key = jax.random.key(seed)
        ks = jax.random.split(key, 8)
        s = lambda k, sh: jax.random.normal(k, sh, jnp.float32) * 0.02
        return dict(x=jax.random.normal(ks[0], (B, T, D), jnp.float32), emb=jax.random.normal(ks[1], (B, TE), jnp.float32), src_mask=jnp.ones((B, T), jnp.float32), norm_w=jnp.ones((D,), jnp.float32), norm_b=jnp.zeros((D,), jnp.float32), q_w=s(ks[2], (D, D)), q_b=jnp.zeros((D,), jnp.float32), k_w=s(ks[3], (D, D)), k_b=jnp.zeros((D,), jnp.float32), v_w=s(ks[4], (D, D)), v_b=jnp.zeros((D,), jnp.float32), emb_w=s(ks[5], (TE, 2 * D)), emb_b=jnp.zeros((2 * D,), jnp.float32), sb_norm_w=jnp.ones((D,), jnp.float32), sb_norm_b=jnp.zeros((D,), jnp.float32), out_w=s(ks[6], (D, D)), out_b=jnp.zeros((D,), jnp.float32))
    _L1_cond_all = _L1_cond_setup()
    _L1_cond_in = {k: v for k, v in _L1_cond_all.items() if k in ('norm_w', 'norm_b', 'q_w', 'q_b', 'k_w', 'k_b', 'v_w', 'v_b', 'emb_w', 'emb_b', 'sb_norm_w', 'sb_norm_b', 'out_w', 'out_b')}
    del _L1_cond_all
    return {'x': x, 'cond_2048': cond_2048, 'mask_BxSx1_fk1': mask_BxSx1_fk1, 'mask_BxS_ff1': mask_BxS_ff1, 'L0_cond_ln_w': _L0_cond_in['ln_w'], 'L0_cond_ln_b': _L0_cond_in['ln_b'], 'L0_cond_Wq': _L0_cond_in['Wq'], 'L0_cond_bq': _L0_cond_in['bq'], 'L0_cond_Wk': _L0_cond_in['Wk'], 'L0_cond_bk': _L0_cond_in['bk'], 'L0_cond_Wv': _L0_cond_in['Wv'], 'L0_cond_bv': _L0_cond_in['bv'], 'L0_cond_W_emb': _L0_cond_in['W_emb'], 'L0_cond_b_emb': _L0_cond_in['b_emb'], 'L0_cond_ln2_w': _L0_cond_in['ln2_w'], 'L0_cond_ln2_b': _L0_cond_in['ln2_b'], 'L0_cond_W_out': _L0_cond_in['W_out'], 'L0_cond_b_out': _L0_cond_in['b_out'], 'L1_cond_norm_w': _L1_cond_in['norm_w'], 'L1_cond_norm_b': _L1_cond_in['norm_b'], 'L1_cond_q_w': _L1_cond_in['q_w'], 'L1_cond_q_b': _L1_cond_in['q_b'], 'L1_cond_k_w': _L1_cond_in['k_w'], 'L1_cond_k_b': _L1_cond_in['k_b'], 'L1_cond_v_w': _L1_cond_in['v_w'], 'L1_cond_v_b': _L1_cond_in['v_b'], 'L1_cond_emb_w': _L1_cond_in['emb_w'], 'L1_cond_emb_b': _L1_cond_in['emb_b'], 'L1_cond_sb_norm_w': _L1_cond_in['sb_norm_w'], 'L1_cond_sb_norm_b': _L1_cond_in['sb_norm_b'], 'L1_cond_out_w': _L1_cond_in['out_w'], 'L1_cond_out_b': _L1_cond_in['out_b']}

def reference(x, cond_2048, mask_BxSx1_fk1, mask_BxS_ff1, L0_cond_ln_w, L0_cond_ln_b, L0_cond_Wq, L0_cond_bq, L0_cond_Wk, L0_cond_bk, L0_cond_Wv, L0_cond_bv, L0_cond_W_emb, L0_cond_b_emb, L0_cond_ln2_w, L0_cond_ln2_b, L0_cond_W_out, L0_cond_b_out, L1_cond_norm_w, L1_cond_norm_b, L1_cond_q_w, L1_cond_q_b, L1_cond_k_w, L1_cond_k_b, L1_cond_v_w, L1_cond_v_b, L1_cond_emb_w, L1_cond_emb_b, L1_cond_sb_norm_w, L1_cond_sb_norm_b, L1_cond_out_w, L1_cond_out_b):
    import jax
    import jax.numpy as jnp

    def _L0_cond_ref(x, emb, src_mask, num_head, ln_w, ln_b, Wq, bq, Wk, bk, Wv, bv, W_emb, b_emb, ln2_w, ln2_b, W_out, b_out):
        import jax, jax.numpy as jnp
        import numpy as np
        B, T, D, H, TE = (4, 512, 256, 8, 512)
        EPS = 1e-05

        def _ln(x, w, b):
            m = jnp.mean(x, axis=-1, keepdims=True)
            v = jnp.mean((x - m) ** 2, axis=-1, keepdims=True)
            return (x - m) * jax.lax.rsqrt(v + EPS) * w + b
        b, t, d = x.shape
        h = num_head
        dh = d // h
        xn = _ln(x, ln_w, ln_b)
        q = xn @ Wq + bq
        k = xn @ Wk + bk + (1.0 - src_mask) * -1000000.0
        q = jax.nn.softmax(q.reshape(b, t, h, dh), axis=-1)
        k = jax.nn.softmax(k.reshape(b, t, h, dh), axis=1)
        v = ((xn @ Wv + bv) * src_mask).reshape(b, t, h, dh)
        att = jnp.einsum('bnhd,bnhl->bhdl', k, v)
        y = jnp.einsum('bnhd,bhdl->bnhl', q, att).reshape(b, t, d)
        emb_out = (jax.nn.silu(emb) @ W_emb + b_emb)[:, None, :]
        scale, shift = jnp.split(emb_out, 2, axis=2)
        hh = _ln(y, ln2_w, ln2_b) * (1.0 + scale) + shift
        hh = jax.nn.silu(hh) @ W_out + b_out
        return x + hh

    def _L1_cond_ref(x, emb, src_mask, norm_w, norm_b, q_w, q_b, k_w, k_b, v_w, v_b, emb_w, emb_b, sb_norm_w, sb_norm_b, out_w, out_b):
        import jax, jax.numpy as jnp
        import numpy as np
        B, T, D, H, TE = (8, 256, 256, 16, 512)
        LN_EPS = 1e-05

        def layer_norm(x, w, b):
            m = jnp.mean(x, axis=-1, keepdims=True)
            v = jnp.var(x, axis=-1, keepdims=True)
            return (x - m) / jnp.sqrt(v + LN_EPS) * w + b
        Bx, Tx, Dx = x.shape
        xn = layer_norm(x, norm_w, norm_b)
        q = (xn @ q_w + q_b).reshape(Bx, Tx, H, -1)
        k = (xn @ k_w + k_b).reshape(Bx, Tx, H, -1)
        att = jnp.einsum('bnhl,bmhl->bnmh', q, k)
        mask = src_mask.reshape(Bx, 1, Tx, 1)
        att = att + (1.0 - mask) * -1000000.0
        att = jax.nn.softmax(att, axis=2)
        v = ((xn @ v_w + v_b) * src_mask[:, :, None]).reshape(Bx, Tx, H, -1)
        y = jnp.einsum('bnmh,bmhl->bnhl', att, v).reshape(Bx, Tx, Dx)
        e = jax.nn.silu(emb) @ emb_w + emb_b
        scale, shift = jnp.split(e[:, None, :], 2, axis=2)
        h = layer_norm(y, sb_norm_w, sb_norm_b) * (1.0 + scale) + shift
        h = jax.nn.silu(h) @ out_w + out_b
        return x + h
    x = _L0_cond_ref(x, cond_2048, mask_BxSx1_fk1, 8, L0_cond_ln_w, L0_cond_ln_b, L0_cond_Wq, L0_cond_bq, L0_cond_Wk, L0_cond_bk, L0_cond_Wv, L0_cond_bv, L0_cond_W_emb, L0_cond_b_emb, L0_cond_ln2_w, L0_cond_ln2_b, L0_cond_W_out, L0_cond_b_out)
    x = _L1_cond_ref(x, cond_2048, mask_BxS_ff1, L1_cond_norm_w, L1_cond_norm_b, L1_cond_q_w, L1_cond_q_b, L1_cond_k_w, L1_cond_k_b, L1_cond_v_w, L1_cond_v_b, L1_cond_emb_w, L1_cond_emb_b, L1_cond_sb_norm_w, L1_cond_sb_norm_b, L1_cond_out_w, L1_cond_out_b)
    return x

_drawn_inputs = setup_inputs


def setup_inputs(seed=0):
    import zlib

    import numpy as np

    out = dict(_drawn_inputs(seed))
    spreads = {'L0_cond_ln_w': (1.0, 0.6),
     'L0_cond_ln_b': (0.0, 0.1),
     'L0_cond_bq': (0.0, 0.8),
     'L0_cond_bk': (0.0, 0.8),
     'L0_cond_bv': (0.0, 0.1),
     'L0_cond_b_emb': (0.0, 0.1),
     'L0_cond_ln2_w': (1.0, 0.2),
     'L0_cond_ln2_b': (0.0, 0.44),
     'L0_cond_b_out': (0.0, 0.1),
     'L1_cond_norm_w': (1.0, 0.536),
     'L1_cond_norm_b': (0.0, 0.1),
     'L1_cond_q_b': (0.0, 0.8),
     'L1_cond_k_b': (0.0, 0.8),
     'L1_cond_v_b': (0.0, 0.1),
     'L1_cond_emb_b': (0.0, 0.275),
     'L1_cond_sb_norm_w': (1.0, 0.2),
     'L1_cond_sb_norm_b': (0.0, 0.415),
     'L1_cond_out_b': (0.0, 0.1)}
    factors = {'L0_cond_Wq': 8.0, 'L0_cond_Wk': 8.0, 'L1_cond_q_w': 3.001, 'L1_cond_k_w': 2.886}
    for name, (base, spread) in spreads.items():
        noise = np.random.default_rng([zlib.crc32(name.encode()), seed]).standard_normal(out[name].shape)
        drawn = base * np.exp(spread * noise) if base else spread * noise
        out[name] = jnp.asarray(drawn.astype(out[name].dtype))
    for name, factor in factors.items():
        out[name] = (out[name] * factor).astype(out[name].dtype)
    return out
```

```python
from contextlib import ExitStack

import concourse.bass as bass
from concourse import mybir

P = 128
B, T, D, TE = 4, 512, 256, 512
NT = T // P
KT = D // P
H0, DH0 = 8, 32
H1, DH1 = 16, 16
G, HG = 4, 4
EPS = 1e-5
MASKED = 1.0e6
N_COLS = 46
SPLIT = 6 * DH1
R_MASK = SPLIT
R_MAX = R_MASK + 3
K_MAX = R_MAX
K_EXP = R_MAX + 2
PARTS_Q = (0, 0, 1, 0, 2, 1)
PARTS_K = (0, 1, 0, 2, 0, 1)

F32 = mybir.dt.float32
BF16 = mybir.dt.bfloat16
ALU = mybir.AluOpType
ACT = mybir.ActivationFunctionType
AX = mybir.AxisListType


class Signal:

    def __init__(self, handle, per_batch):
        self.handle, self.per_batch = handle, per_batch

    def wait(self, engine, b, k):
        engine.wait_ge(self.handle, b * self.per_batch + k)

    def all_before(self, engine, b):
        if isinstance(b, int) and b == 0:
            return
        engine.wait_ge(self.handle, b * self.per_batch)


class Chain:

    def __init__(self, engine, steps, b):
        self.engine, self.steps, self.b, self.k = engine, steps, b, 0

    def done(self, instruction):
        self.k += 1
        instruction.then_inc(self.steps.handle, 1)

    def __call__(self, instruction):
        self.done(instruction)
        self.steps.wait(self.engine, self.b, self.k)


def build(nc, a, out):
    with ExitStack() as ctx:
        def sb(name, shape, dt=F32):
            return ctx.enter_context(nc.sbuf_tensor(name, shape, dt))

        def sem(name):
            return ctx.enter_context(nc.semaphore(name))

        def counted(name, per_batch):
            return Signal(sem(name), per_batch)

        consts = sb("consts", [P, 2 * P])
        ident = consts[:, 0:P]
        block_diag = consts[:, P:2 * P]
        ident_bf = sb("ident_bf", [P, P], BF16)
        w_qv0 = sb("w_qv0", [P, KT, 2 * D])
        w_k0 = sb("w_k0", [P, KT, D])
        w_out = [sb(f"w_out{i}", [P, KT, D]) for i in range(2)]
        w_q1 = sb("w_q1", [P, KT, D])
        w_k1 = sb("w_k1", [P, KT, D])
        w_v1 = sb("w_v1", [P, KT, D])
        probs = sb("probs", [P, 4, 2, T])
        w_emb = probs[:, :, :, :].rearrange("p a b t -> p (a b t)").rearrange("p (i c n) -> p i c n", i=2, c=TE // P)
        cols = sb("cols", [P, N_COLS])
        pair = lambda k: cols[:, k:k + 2 * KT].rearrange("p (i f) -> p i f", f=KT)
        ln_w, ln_b, ln2_w, ln2_b = (pair(2 * KT * k) for k in range(4))
        b_emb = cols[:, 16:24].rearrange("p (i o) -> p i o", o=4)
        bias_col_in = cols[:, 24:30].rearrange("p (i f) -> p i f", f=KT)
        cond = cols[:, 30:46].rearrange("p (c b) -> p c b", b=B)
        ln_b_wide = sb("ln_b_wide", [P, 2, KT, P])
        bias_col = sb("bias_col", [P, 3, KT])
        vec = sb("vec", [P, 5 * D])
        bias_qv0_in = vec[:, 0:2 * D]
        bias_v1_in = vec[:, 2 * D:3 * D]
        bias_out = vec[:, 3 * D:5 * D].rearrange("p (i d) -> p i d", i=2)
        bias_qv0 = sb("bias_qv0", [P, 2 * D])
        bias_v1 = sb("bias_v1", [P, D])
        cond_tanh = sb("cond_tanh", [P, TE // P, B])
        cond_t = sb("cond_t", [P, TE // P, B])
        emb = sb("emb", [P, 2, 4, B])
        emb_s1 = sb("emb_s1", [P, 2, KT, B])
        emb_t = sb("emb_t", [P, 2, KT, B])
        by_batch = sb("by_batch", [P, 16, B])
        film = by_batch[:, 0:8, :].rearrange("p (i c f) b -> p i c f b", i=2, c=2)
        minus_half = sb("minus_half", [P, NT])
        eps_col = sb("eps_col", [P, NT])

        x = sb("x", [P, NT, D])
        x_plus = sb("x_plus", [P, NT, D])
        x1 = sb("x1", [P, NT, D])
        res = x1
        xn = sb("xn", [P, NT, D])
        xn_t = sb("xn_t", [P, KT, T])
        stats = sb("stats", [P, NT, 6])
        spare = sb("spare", [P, 4])
        mean_var = sb("mean_var", [P, NT, 2])
        var_eps = sb("var_eps", [P, NT])
        rstd = sb("rstd", [P, NT])
        now = sb("now", [P, 16])
        film_now = now[:, 0:8].rearrange("p (i c f) -> p i c f", i=2, c=2)
        mask0_col, mask1_col = now[:, 8:12], now[:, 12:16]
        mask0_wide = sb("mask0_wide", [P, T])
        mask1_rows = sb("mask1_rows", [B, T])
        mask1_rest = sb("mask1_rest", [B, 3, T])
        mask1_part = sb("mask1_part", [B, 3, T], BF16)
        mask1_line = sb("mask1_line", [1, B * 3, T], BF16)
        k_exp = sb("k_exp", [P, KT, T])
        k_negmax = sb("k_negmax", [P, KT])
        k_sum = sb("k_sum", [P, KT])
        k_rec = sb("k_rec", [P, KT])
        o_sb = sb("o_sb", [P, 2, T])
        k_tok = o_sb[:, :, :].rearrange("p a (n d) -> p (a n) d", d=D)
        qv = sb("qv", [P, NT, 2 * D])
        q_max = sb("q_max", [P, NT, H0])
        q_exp = sb("q_exp", [P, NT, D])
        q_sum = sb("q_sum", [P, NT * H0])
        q_rec = sb("q_rec", [P, NT * H0])
        q_t = sb("q_t", [P, KT, T])
        att = sb("att", [P, KT, P])
        y = sb("y", [P, NT, D])
        half_h = sb("half_h", [P, KT, T])
        tanh_h = sb("tanh_h", [P, KT, T])
        qk = sb("qk", [P, 2, KT, T])
        qk_rest = sb("qk_rest", [P, 2, KT, T])
        qk_part = sb("qk_part", [P, 3, 2, KT, T], BF16)
        q_stack = sb("q_stack", [P, H1, T], BF16)
        k_stack = sb("k_stack", [P, H1, T], BF16)
        v_sum = sb("v_sum", [P, NT, D])
        v1 = sb("v1", [P, NT, H1, 32])
        row_max = sb("row_max", [P, G, NT, HG])
        max_rest = sb("max_rest", [P, G, NT, HG])
        max_part = sb("max_part", [P, G, NT, 2, HG], BF16)
        max_row = sb("max_row", [2 * HG, G, T], BF16)
        o_rec = sb("o_rec", [P, G, NT, HG])

        ps = ctx.enter_context(nc.psum_tensor("ps", [P, 8, 512], F32))
        scratch = nc.dram_tensor("scratch", (3, 2, D, T), BF16, kind="Internal").ap()

        s_weights = sem("s_weights")
        s_consts = sem("s_consts")
        s_tanh_c = sem("s_tanh_c")
        s_cond_t = sem("s_cond_t")
        s_emb_ps = sem("s_emb_ps")
        s_bias_ps = sem("s_bias_ps")
        s_ident_bf = sem("s_ident_bf")
        s_wide = sem("s_wide")
        s_setup = sem("s_setup")
        s_setup_pool = sem("s_setup_pool")
        s_dve0 = sem("s_dve0")
        s_mask_parts = sem("s_mask_parts")
        s_mask_line = sem("s_mask_line")

        x_loaded = counted("x_loaded", 16)
        masks_loaded = counted("masks_loaded", 16)
        stats_ready = counted("stats_ready", 4)
        rstd_ready = counted("rstd_ready", 4)
        xn_ready = counted("xn_ready", 16)
        tp_ready = counted("tp_ready", 4)
        xnt_ready = counted("xnt_ready", 2)
        k0_ps = counted("k0_ps", KT)
        qv_ps = counted("qv_ps", NT)
        k_max_ready = counted("k_max_ready", KT)
        k_exp_ready = counted("k_exp_ready", KT)
        q_cent_ready = counted("q_cent_ready", 1)
        q_exp_ready = counted("q_exp_ready", 1)
        v0_ready = counted("v0_ready", 1)
        k_tok_ps = counted("k_tok_ps", 1)
        k_tok_ready = counted("k_tok_ready", 1)
        q_t_ps = counted("q_t_ps", 1)
        q_t_ready = counted("q_t_ready", 1)
        att_ps = counted("att_ps", 1)
        att_ready = counted("att_ready", 1)
        y_ps = counted("y_ps", 1)
        half_ready = counted("half_ready", 2)
        tanh_ready = counted("tanh_ready", 2)
        silu_ready = counted("silu_ready", 2)
        out_ps = counted("out_ps", 2)
        x_plus_ready = counted("x_plus_ready", 2)
        x1_ready = counted("x1_ready", 1)
        res_ready = counted("res_ready", 1)
        q1_ps = counted("q1_ps", 1)
        k1_ps = counted("k1_ps", 1)
        v1_ps = counted("v1_ps", 1)
        qk_ready = counted("qk_ready", 2)
        part0_ready = counted("part0_ready", 2)
        rest_ready = counted("rest_ready", 2)
        part1_ready = counted("part1_ready", 2)
        part2_ready = counted("part2_ready", 2)
        stacks_loaded = counted("stacks_loaded", 16 * (12 + 3))
        part_kept = {(p, i): counted(f"part_kept{p}{i}", 16) for p in range(3) for i in range(2)}
        v1_ready = counted("v1_ready", 1)
        a_ps = counted("a_ps", G * HG * NT)
        a_read = counted("a_read", G * HG * NT)
        max_part_ready = counted("max_part_ready", G)
        max_row_ps = counted("max_row_ps", G)
        max_row_ready = counted("max_row_ready", G)
        max_loaded = [counted(f"max_loaded{g}", 32) for g in range(G)]
        s_ps = counted("s_ps", G * NT * 2)
        probs_ready = counted("probs_ready", G * NT * 2)
        probs_used = counted("probs_used", G * NT)
        o_copied = counted("o_copied", G)
        o_tp_ps = counted("o_tp_ps", G)
        y1_done = counted("y1_done", G)
        stored = counted("stored", 16)
        dve_step = counted("dve_step", 27)
        act_step = counted("act_step", 2)
        pool_step = counted("pool_step", 4)

        N_WEIGHTS = 10
        N_CONSTS = 5
        SETUP_POOL = 6

        block = ctx.enter_context(nc.Block())

        rows = lambda v: v.rearrange("(c p) n -> p c n", p=P)

        @block.sync
        def _(sp):
            w = lambda dst, src: sp.dma_start(dst, src).then_inc(s_weights, 16)
            c = lambda dst, src: sp.dma_start(dst, src).then_inc(s_consts, 16)
            c(consts[:, :], a["consts"])
            c(cols[:, :], a["cols"])
            c(by_batch[:, 8:16, :], a["mask_cols"])
            w(w_k0[:, :, :], rows(a["L0_cond_Wk"]))
            w(w_qv0[:, :, 0:D], rows(a["L0_cond_Wq"]))
            w(w_qv0[:, :, D:2 * D], rows(a["L0_cond_Wv"]))
            c(mask1_rows[:, :], a["mask_BxS_ff1"])
            c(vec[:, :], a["vectors"].rearrange("(a n) -> a n", a=1).to_broadcast([P, 5 * D]))
            w(w_q1[:, :, :], rows(a["L1_cond_q_w"]))
            w(w_k1[:, :, :], rows(a["L1_cond_k_w"]))
            w(w_v1[:, :, :], rows(a["L1_cond_v_w"]))
            w(w_emb[:, 0, :, :], rows(a["L0_cond_W_emb"]))
            w(w_emb[:, 1, :, :], rows(a["L1_cond_emb_w"]))
            w(w_out[0][:, :, :], rows(a["L0_cond_W_out"]))
            w(w_out[1][:, :, :], rows(a["L1_cond_out_w"]))
            sp.wait_ge(s_mask_parts, 1)
            sp.dma_start(mask1_line[:, :, :], mask1_part[:, :, :]).then_inc(s_mask_line, 16)
            def batch(b):
                res_ready.all_before(sp, b)
                sp.dma_start(x[:, :, :], a["x"][b].rearrange("(n p) d -> p n d", p=P)).then_inc(x_loaded.handle, 16)
                m0 = a["mask_BxSx1_fk1"][b].rearrange("t a -> a t")
                ml = masks_loaded.handle
                sp.dma_start(mask0_wide[:, :], m0.to_broadcast([P, T])).then_inc(ml, 16)
                sp.wait_ge(s_mask_line, 16)
                probs_ready.all_before(sp, b)
                for part in range(3):
                    r = R_MASK + part
                    sp.dma_start(k_stack[r:r + 1, :, :], mask1_line[0:1, bass.ds(b * 3 + part, 1), :].to_broadcast([1, H1, T])
                                 ).then_inc(stacks_loaded.handle, 16)
                for part, ready in ((0, part0_ready), (1, part1_ready), (2, part2_ready)):
                    for side, (stack, order) in enumerate(((q_stack, PARTS_Q), (k_stack, PARTS_K))):
                        ready.wait(sp, b, side + 1)
                        sp.dma_start(scratch[part, side].rearrange("(f p) t -> p f t", p=P), qk_part[:, part, side, :, :]
                                     ).then_inc(part_kept[part, side].handle, 16)
                        part_kept[part, side].wait(sp, b, 16)
                        for j in range(6):
                            if order[j] == part:
                                sp.dma_start(stack[j * DH1:(j + 1) * DH1, :, :], scratch[part, side].rearrange("(h l) t -> l h t", l=DH1)
                                             ).then_inc(stacks_loaded.handle, 16)
                for g in range(G):
                    max_row_ready.wait(sp, b, g + 1)
                    for part in range(2):
                        r = R_MAX + part
                        sp.dma_start(q_stack[r:r + 1, g * HG:(g + 1) * HG, :],
                                     max_row[part * HG:(part + 1) * HG, g, :]).then_inc(max_loaded[g].handle, 16)
                res_ready.wait(sp, b, 1)
                sp.dma_start(out[b].rearrange("(n p) d -> p n d", p=P), res[:, :, :]).then_inc(stored.handle, 16)

            batch(0)
            with sp.Fori(1, B) as b:
                batch(b)
            stored.wait(sp, B - 1, 16)

        @block.gpsimd
        def _(pool):
            k0 = [0]

            def link(instruction):
                k0[0] += 1
                instruction.then_inc(s_setup_pool, 1)
                pool.wait_ge(s_setup_pool, k0[0])

            link(nc.gpsimd.memset(minus_half[:, :], -0.5))
            link(nc.gpsimd.memset(eps_col[:, :], EPS))
            link(nc.gpsimd.memset(v1[:, :, :, :], 0.0))
            link(nc.gpsimd.memset(v1[:, :, :, DH1:DH1 + 1], 1.0))
            link(nc.gpsimd.memset(q_stack[SPLIT:P, :, :], 1.0))
            link(nc.gpsimd.memset(k_stack[SPLIT:P, :, :], 1.0))
            assert k0[0] == SETUP_POOL
            pool.wait_ge(s_consts, 16 * N_CONSTS)
            link(nc.gpsimd.tensor_scalar(mask1_rest[:, 0, :], mask1_rows[:, :], 1.0, MASKED, ALU.subtract, ALU.mult))
            link(nc.gpsimd.tensor_copy(mask1_part[:, 0, :], mask1_rest[:, 0, :]))
            link(nc.gpsimd.tensor_tensor(mask1_rest[:, 1, :], mask1_rest[:, 0, :], mask1_part[:, 0, :], ALU.subtract))
            link(nc.gpsimd.tensor_copy(mask1_part[:, 1, :], mask1_rest[:, 1, :]))
            link(nc.gpsimd.tensor_tensor(mask1_rest[:, 2, :], mask1_rest[:, 1, :], mask1_part[:, 1, :], ALU.subtract))
            nc.gpsimd.tensor_copy(mask1_part[:, 2, :], mask1_rest[:, 2, :]).then_inc(s_mask_parts, 1)
            def batch(b):
                step = Chain(pool, pool_step, b)

                def norm(i):
                    stats_ready.wait(pool, b, i + 1)
                    step(nc.gpsimd.tensor_tensor(var_eps[:, :], mean_var[:, :, 1], eps_col[:, :], ALU.add))
                    nc.gpsimd.tensor_tensor(rstd[:, :], var_eps[:, :], minus_half[:, :], ALU.pow).then_inc(rstd_ready.handle, 1)

                norm(0)
                x_loaded.wait(pool, b, 16)
                bias0 = bias_out[:, 0:1, :].to_broadcast([P, NT, D])
                bias1 = bias_out[:, 1:2, :].to_broadcast([P, NT, D])
                nc.gpsimd.tensor_tensor(x_plus[:, :, :], x[:, :, :], bias0, ALU.add).then_inc(x_plus_ready.handle, 1)
                norm(1)
                norm(2)
                x1_ready.wait(pool, b, 1)
                nc.gpsimd.tensor_tensor(x_plus[:, :, :], x1[:, :, :], bias1, ALU.add).then_inc(x_plus_ready.handle, 1)
                norm(3)
                assert step.k == pool_step.per_batch, step.k

            batch(0)
            with pool.Fori(1, B) as b:
                batch(b)

        @block.scalar
        def _(act):
            act.wait_ge(s_consts, 16 * N_CONSTS)
            nc.scalar.activation(cond_tanh[:, :, :], cond, ACT.Tanh, scale=0.5).then_inc(s_tanh_c, 1)
            def batch(b):
                step = Chain(act, act_step, b)

                def take_xn_t(i):
                    tp_ready.wait(act, b, 2 * i + 1)
                    nc.scalar.copy(xn_t[:, :, :], ps[:, 0:KT, :]).then_inc(xnt_ready.handle, 1)

                def modulate(i):
                    tp_ready.wait(act, b, 2 * i + 2)
                    for f in range(KT):
                        last = nc.scalar.activation(half_h[:, f, :], ps[:, f, :], ACT.Identity,
                                                    bias=film_now[:, i, 1, f:f + 1], scale=film_now[:, i, 0, f:f + 1])
                    last.then_inc(half_ready.handle, 1)
                    half_ready.wait(act, b, i + 1)
                    nc.scalar.activation(tanh_h[:, :, :], half_h[:, :, :], ACT.Tanh).then_inc(tanh_ready.handle, 1)

                take_xn_t(0)
                for f in range(KT):
                    k_max_ready.wait(act, b, f + 1)
                    nc.scalar.activation(k_exp[:, f, :], k_exp[:, f, :], ACT.Exp, bias=k_negmax[:, f:f + 1],
                                         accum_out=k_sum[:, f:f + 1]).then_inc(k_exp_ready.handle, 1)
                q_cent_ready.wait(act, b, 1)
                nc.scalar.activation(q_exp[:, :, :], qv[:, :, 0:D], ACT.Exp).then_inc(q_exp_ready.handle, 1)
                k_tok_ps.wait(act, b, 1)
                nc.scalar.copy(k_tok[:, :, :], ps[:, 0:2, :]).then_inc(k_tok_ready.handle, 1)
                q_t_ps.wait(act, b, 1)
                nc.scalar.copy(q_t[:, :, :], ps[:, 2:4, :]).then_inc(q_t_ready.handle, 1)
                modulate(0)

                take_xn_t(1)
                for side, (src, bank) in enumerate(((q1_ps, 2), (k1_ps, 4))):
                    src.wait(act, b, 1)
                    for f in range(KT):
                        last = nc.scalar.activation(qk[:, side, f, :], ps[:, bank + f, :], ACT.Identity,
                                                    bias=bias_col[:, 1 + side, f:f + 1])
                    last.then_inc(qk_ready.handle, 1)
                    qk_ready.wait(act, b, side + 1)
                    nc.scalar.copy(qk_part[:, 0, side, :, :], qk[:, side, :, :]).then_inc(part0_ready.handle, 1)
                for side in range(2):
                    rest_ready.wait(act, b, side + 1)
                    nc.scalar.copy(qk_part[:, 1, side, :, :], qk_rest[:, side, :, :]).then_inc(part1_ready.handle, 1)

                def exp_step(s):
                    for pair in range(2):
                        u = 2 * s + pair
                        s_ps.wait(act, b, u + 1)
                        if s >= 2:
                            probs_used.wait(act, b, s - 1)
                        else:
                            probs_used.all_before(act, b)
                        nc.scalar.activation(probs[:, u % 4, :, :], ps[:, 2 * pair:2 * pair + 2, :], ACT.Exp
                                             ).then_inc(probs_ready.handle, 1)

                def take_o(g):
                    probs_used.wait(act, b, NT * (g + 1))
                    if g >= 2:
                        o_tp_ps.wait(act, b, g - 1)
                    nc.scalar.copy(o_sb[:, g % 2, :], ps[:, 6, :]).then_inc(o_copied.handle, 1)

                for s in range(G * NT):
                    exp_step(s)
                    if s % NT == 0 and s:
                        take_o(s // NT - 1)
                take_o(G - 1)
                modulate(1)

            batch(0)
            with act.Fori(1, B) as b:
                batch(b)

        @block.vector
        def _(dve):
            k0 = [0]

            def link(instruction):
                k0[0] += 1
                instruction.then_inc(s_dve0, 1)
                dve.wait_ge(s_dve0, k0[0])

            dve.wait_ge(s_consts, 16 * N_CONSTS)
            nc.vector.tensor_copy(ident_bf[:, :], ident).then_inc(s_ident_bf, 1)
            nc.vector.tensor_copy(ln_b_wide[:, :, :, :], ln_b[:, :, :].unsqueeze(3).to_broadcast([P, 2, KT, P])
                                  ).then_inc(s_wide, 1)
            dve.wait_ge(s_tanh_c, 1)
            link(nc.vector.scalar_tensor_tensor(cond_t[:, :, :], cond_tanh[:, :, :], 1.0, cond, ALU.add, ALU.mult))
            nc.vector.tensor_scalar(cond_t[:, :, :], cond_t[:, :, :], 0.5, None, ALU.mult).then_inc(s_cond_t, 1)
            dve.wait_ge(s_bias_ps, 1)
            nc.vector.tensor_tensor(bias_col[:, :, :], ps[:, 0, 0:3 * KT].rearrange("p (i f) -> p i f", f=KT),
                                    bias_col_in[:, :, :], ALU.add)
            nc.vector.tensor_tensor(bias_qv0[:, :], ps[:, 1, :], bias_qv0_in, ALU.add)
            nc.vector.tensor_tensor(bias_v1[:, :], ps[:, 2, 0:D], bias_v1_in, ALU.add)
            for f in range(KT):
                for i, wt in ((0, w_k0), (0, w_qv0), (1, w_q1), (1, w_k1), (1, w_v1)):
                    last = nc.vector.tensor_scalar(wt[:, f, :], wt[:, f, :], ln_w[:, i, f:f + 1], None, ALU.mult)
            link(last)
            dve.wait_ge(s_emb_ps, 1)
            link(nc.vector.tensor_tensor(emb[:, :, :, :], ps[:, 4, 0:2 * 4 * B].rearrange("p (i o b) -> p i o b", i=2, o=4),
                                         b_emb[:, :, :].unsqueeze(3).to_broadcast([P, 2, 4, B]), ALU.add))
            link(nc.vector.tensor_scalar(emb_s1[:, :, :, :], emb[:, :, 0:KT, :], 1.0, 0.5, ALU.add, ALU.mult))
            nc.vector.tensor_tensor(film[:, :, 0, :, :], emb_s1[:, :, :, :],
                                    ln2_w[:, :, :].unsqueeze(3).to_broadcast([P, 2, KT, B]), ALU.mult)
            link(nc.vector.tensor_tensor(emb_t[:, :, :, :], emb_s1[:, :, :, :],
                                         ln2_b[:, :, :].unsqueeze(3).to_broadcast([P, 2, KT, B]), ALU.mult))
            for i in range(2):
                last = nc.vector.scalar_tensor_tensor(film[:, i, 1, :, :], emb[:, i, KT:2 * KT, :], 0.5,
                                                      emb_t[:, i, :, :], ALU.mult, ALU.add)
            last.then_inc(s_setup, 1)
            dve.wait_ge(s_setup, 1)
            dve.wait_ge(s_setup_pool, SETUP_POOL)

            def batch(b):
                step = Chain(dve, dve_step, b)

                def norm(i, src):
                    for n in range(NT):
                        last = nc.vector.bn_stats(stats[:, n, :], src[:, n, :])
                    step(last)
                    nc.vector.tensor_copy(spare[:, i:i + 1], stats[:, 0, 0:1])
                    for n in range(NT):
                        last = nc.vector.bn_aggr(mean_var[:, n, :], stats[:, n, :])
                    last.then_inc(stats_ready.handle, 1)
                    stats_ready.wait(dve, b, i + 1)
                    rstd_ready.wait(dve, b, i + 1)
                    for n in range(NT):
                        nc.vector.tensor_scalar(xn[:, n, :], src[:, n, :], mean_var[:, n, 0:1], rstd[:, n:n + 1],
                                                ALU.subtract, ALU.mult).then_inc(xn_ready.handle, 1)

                def silu(i):
                    tanh_ready.wait(dve, b, i + 1)
                    nc.vector.scalar_tensor_tensor(tanh_h[:, :, :], tanh_h[:, :, :], 1.0, half_h[:, :, :],
                                                   ALU.add, ALU.mult).then_inc(silu_ready.handle, 1)

                res_ready.all_before(dve, b)
                step(nc.vector.tensor_copy(now[:, :], by_batch[:, :, bass.ds(b, 1)].rearrange("p a b -> p (a b)")))
                x_loaded.wait(dve, b, 16)
                norm(0, x)
                masks_loaded.wait(dve, b, 16)
                step(nc.vector.tensor_scalar(mask0_wide[:, :], mask0_wide[:, :], 1.0, MASKED, ALU.subtract, ALU.mult))
                for f in range(KT):
                    k0_ps.wait(dve, b, f + 1)
                    step(nc.vector.scalar_tensor_tensor(k_exp[:, f, :], ps[:, 2 + f, :], bias_col[:, 0, f:f + 1],
                                                        mask0_wide[:, :], ALU.add, ALU.add))
                    nc.vector.tensor_reduce(k_negmax[:, f:f + 1], k_exp[:, f, :], AX.X, ALU.max, negate=True
                                            ).then_inc(k_max_ready.handle, 1)
                for n in range(NT):
                    qv_ps.wait(dve, b, n + 1)
                    last = nc.vector.tensor_tensor(qv[:, n, :], ps[:, 4 + n, :], bias_qv0[:, :], ALU.add)
                step(last)
                q_in = qv[:, :, 0:D].rearrange("p n (h l) -> p n h l", l=DH0)
                step(nc.vector.tensor_reduce(q_max[:, :, :], q_in, AX.X, ALU.max))
                for n in range(NT):
                    last = nc.vector.tensor_tensor(q_in[:, n], q_in[:, n],
                                                   q_max[:, n, :].unsqueeze(2).to_broadcast([P, H0, DH0]), ALU.subtract)
                last.then_inc(q_cent_ready.handle, 1)
                for n in range(NT):
                    last = nc.vector.tensor_scalar(qv[:, n, D:2 * D], qv[:, n, D:2 * D], mask0_col[:, n:n + 1], None, ALU.mult)
                last.then_inc(v0_ready.handle, 1)
                q_exp_ready.wait(dve, b, 1)
                step(nc.vector.tensor_reduce(q_sum[:, :], q_exp[:, :, :].rearrange("p n (h l) -> p (n h) l", l=DH0), AX.X, ALU.add))
                step(nc.vector.reciprocal(q_rec[:, :], q_sum[:, :]))
                k_exp_ready.wait(dve, b, KT)
                step(nc.vector.reciprocal(k_rec[:, :], k_sum[:, :]))
                att_ps.wait(dve, b, 1)
                for f in range(KT):
                    last = nc.vector.scalar_tensor_tensor(att[:, f, :], ps[:, 4, f * P:(f + 1) * P], k_rec[:, f:f + 1],
                                                          block_diag, ALU.mult, ALU.mult)
                last.then_inc(att_ready.handle, 1)
                y_ps.wait(dve, b, 1)
                step(nc.vector.tensor_tensor(y[:, :, :].rearrange("p n (h l) -> p (n h) l", l=DH0),
                                             ps[:, 5:7, :].rearrange("p n (h l) -> p (n h) l", l=DH0),
                                             q_rec[:, :].unsqueeze(2).to_broadcast([P, NT * H0, DH0]), ALU.mult))
                norm(1, y)
                silu(0)
                x_plus_ready.wait(dve, b, 1)
                out_ps.wait(dve, b, 1)
                stored.all_before(dve, b)
                nc.vector.tensor_tensor(x1[:, :, :], ps[:, 2:4, :].rearrange("p a (n d) -> p (a n) d", d=D), x_plus[:, :, :],
                                        ALU.add).then_inc(x1_ready.handle, 1)
                x1_ready.wait(dve, b, 1)

                norm(2, x1)
                for side in range(2):
                    part0_ready.wait(dve, b, side + 1)
                    nc.vector.tensor_tensor(qk_rest[:, side, :, :], qk[:, side, :, :], qk_part[:, 0, side, :, :],
                                            ALU.subtract).then_inc(rest_ready.handle, 1)
                for side in range(2):
                    part1_ready.wait(dve, b, side + 1)
                    nc.vector.tensor_tensor(qk_part[:, 2, side, :, :], qk_rest[:, side, :, :], qk_part[:, 1, side, :, :],
                                            ALU.subtract).then_inc(part2_ready.handle, 1)
                v1_ps.wait(dve, b, 1)
                step(nc.vector.tensor_tensor(v_sum[:, :, :], ps[:, 6:8, :].rearrange("p a (n d) -> p (a n) d", d=D),
                                             bias_v1[:, :].unsqueeze(1).to_broadcast([P, NT, D]), ALU.add))
                for n in range(NT):
                    last = nc.vector.tensor_scalar(v1[:, n, :, 0:DH1], v_sum[:, n, :].rearrange("p (h l) -> p h l", l=DH1),
                                                   mask1_col[:, n:n + 1], None, ALU.mult)
                last.then_inc(v1_ready.handle, 1)

                def maxima(g, hh):
                    for n in range(NT):
                        i = (g * HG + hh) * NT + n
                        a_ps.wait(dve, b, i + 1)
                        nc.vector.tensor_reduce(row_max[:, g, n, hh:hh + 1], ps[:, 4 + i % 2, :], AX.X, ALU.max
                                                ).then_inc(a_read.handle, 1)

                def split_max(g):
                    a_read.wait(dve, b, (g + 1) * HG * NT)
                    step(nc.vector.tensor_scalar(max_part[:, g, :, 0, :], row_max[:, g, :, :], -1.0, None, ALU.mult))
                    step(nc.vector.tensor_tensor(max_rest[:, g, :, :], row_max[:, g, :, :], max_part[:, g, :, 0, :], ALU.add))
                    nc.vector.tensor_scalar(max_part[:, g, :, 1, :], max_rest[:, g, :, :], -1.0, None, ALU.mult
                                            ).then_inc(max_part_ready.handle, 1)

                def take_max_row(g):
                    max_row_ps.wait(dve, b, g + 1)
                    nc.vector.tensor_copy(max_row[:, g, :], ps[0:2 * HG, 7, 0:T // 2].bitcast(BF16)
                                          ).then_inc(max_row_ready.handle, 1)

                def normalise(g):
                    o_tp_ps.wait(dve, b, g + 1)
                    o = ps[:, 7, :].rearrange("p (n h c) -> p n h c", n=NT, h=HG)
                    step(nc.vector.reciprocal(o_rec[:, g, :, :], o[:, :, :, DH1]))
                    nc.vector.tensor_tensor(
                        y[:, :, g * HG * DH1:(g + 1) * HG * DH1].rearrange("p n (h l) -> p n h l", l=DH1),
                        o[:, :, :, 0:DH1], o_rec[:, g, :, :].unsqueeze(3).to_broadcast([P, NT, HG, DH1]), ALU.mult
                    ).then_inc(y1_done.handle, 1)

                for g in range(2):
                    for hh in range(HG):
                        maxima(g, hh)
                    split_max(g)
                    take_max_row(g)
                for s in range(G * NT):
                    g, m = divmod(s, NT)
                    if m == 0 and 1 <= g < G - 1:
                        take_max_row(g + 1)
                    if m == 1 and g >= 1:
                        normalise(g - 1)
                    if g + 2 < G:
                        maxima(g + 2, m)
                        if m == NT - 1:
                            split_max(g + 2)
                normalise(G - 1)
                y1_done.wait(dve, b, G)
                norm(3, y)
                silu(1)
                x_plus_ready.wait(dve, b, 2)
                out_ps.wait(dve, b, 2)
                nc.vector.tensor_tensor(res[:, :, :], ps[:, 2:4, :].rearrange("p a (n d) -> p (a n) d", d=D), x_plus[:, :, :],
                                        ALU.add).then_inc(res_ready.handle, 1)
                assert step.k == dve_step.per_batch, step.k

            batch(0)
            with dve.Fori(1, B) as b:
                batch(b)

        @block.tensor
        def _(pe):
            mm = nc.tensor.matmul
            pe.wait_ge(s_weights, 16 * N_WEIGHTS)
            pe.wait_ge(s_wide, 1)
            for i, (layer, wt) in enumerate(((0, w_k0), (1, w_q1), (1, w_k1))):
                for o in range(KT):
                    for f in range(KT):
                        mm(ps[:, 0, i * KT + o:i * KT + o + 1], wt[:, f, o * P:(o + 1) * P], ln_b[:, layer, f:f + 1],
                           start=(f == 0), stop=(f == KT - 1))
            for f in range(KT):
                mm(ps[:, 1, :], ln_b_wide[:, 0, f, :], w_qv0[:, f, :], start=(f == 0), stop=(f == KT - 1))
            for f in range(KT):
                last = mm(ps[:, 2, 0:D], ln_b_wide[:, 1, f, :], w_v1[:, f, :], start=(f == 0), stop=(f == KT - 1))
            last.then_inc(s_bias_ps, 1)
            pe.wait_ge(s_cond_t, 1)
            for i in range(2):
                for o in range(4):
                    for c in range(TE // P):
                        q = (i * 4 + o) * B
                        last = mm(ps[:, 4, q:q + B], w_emb[:, i, c, o * P:(o + 1) * P], cond_t[:, c, :],
                                  start=(c == 0), stop=(c == TE // P - 1))
            last.then_inc(s_emb_ps, 1)
            pe.wait_ge(s_ident_bf, 1)
            pe.wait_ge(s_setup, 1)
            pe.wait_ge(s_setup_pool, SETUP_POOL)

            def batch(b):
                def turn(i):
                    for n in range(NT):
                        xn_ready.wait(pe, b, i * NT + n + 1)
                        for f in range(KT):
                            last = nc.tensor.transpose(ps[:, f, n * P:(n + 1) * P], xn[:, n, f * P:(f + 1) * P], ident)
                    last.then_inc(tp_ready.handle, 1)

                def features(bank, wt):
                    for o in range(KT):
                        for f in range(KT):
                            last = mm(ps[:, bank + o, :], wt[:, f, o * P:(o + 1) * P], xn_t[:, f, :],
                                      start=(f == 0), stop=(f == KT - 1))
                        yield last

                def tokens(bank, left, wt, width):
                    per = 512 // width
                    for n in range(NT):
                        c = (n % per) * width
                        for f in range(KT):
                            last = mm(ps[:, bank + n // per, c:c + width], left[:, f, n * P:(n + 1) * P], wt[:, f, 0:width],
                                      start=(f == 0), stop=(f == KT - 1))
                        yield last

                def project_out(i):
                    silu_ready.wait(pe, b, i + 1)
                    for last in tokens(2, tanh_h, w_out[i], D):
                        pass
                    last.then_inc(out_ps.handle, 1)

                res_ready.all_before(pe, b)
                turn(0)
                xnt_ready.wait(pe, b, 1)
                for last in features(2, w_k0):
                    last.then_inc(k0_ps.handle, 1)
                for last in tokens(4, xn_t, w_qv0, 2 * D):
                    last.then_inc(qv_ps.handle, 1)
                k_exp_ready.wait(pe, b, KT)
                for n in range(NT):
                    for f in range(KT):
                        c = (n % 2) * D + f * P
                        last = nc.tensor.transpose(ps[:, n // 2, c:c + P], k_exp[:, f, n * P:(n + 1) * P], ident)
                last.then_inc(k_tok_ps.handle, 1)
                q_exp_ready.wait(pe, b, 1)
                for f in range(KT):
                    for n in range(NT):
                        last = nc.tensor.transpose(ps[:, 2 + f, n * P:(n + 1) * P], q_exp[:, n, f * P:(f + 1) * P], ident)
                last.then_inc(q_t_ps.handle, 1)
                k_tok_ready.wait(pe, b, 1)
                v0_ready.wait(pe, b, 1)
                for f in range(KT):
                    for n in range(NT):
                        last = mm(ps[:, 4, f * P:(f + 1) * P], k_tok[:, n, f * P:(f + 1) * P], qv[:, n, D + f * P:D + (f + 1) * P],
                                  start=(n == 0), stop=(n == NT - 1))
                last.then_inc(att_ps.handle, 1)
                att_ready.wait(pe, b, 1)
                q_t_ready.wait(pe, b, 1)
                for n in range(NT):
                    for f in range(KT):
                        c = (n % 2) * D + f * P
                        last = mm(ps[:, 5 + n // 2, c:c + P], q_t[:, f, n * P:(n + 1) * P], att[:, f, :], start=True, stop=True)
                last.then_inc(y_ps.handle, 1)
                turn(1)
                project_out(0)

                turn(2)
                xnt_ready.wait(pe, b, 2)
                for last in features(2, w_q1):
                    pass
                last.then_inc(q1_ps.handle, 1)
                for last in features(4, w_k1):
                    pass
                last.then_inc(k1_ps.handle, 1)
                for last in tokens(6, xn_t, w_v1, D):
                    pass
                last.then_inc(v1_ps.handle, 1)

                def maxima(g, hh):
                    h = g * HG + hh
                    for n in range(NT):
                        i = h * NT + n
                        if i >= 2:
                            a_read.wait(pe, b, i - 1)
                        mm(ps[:, 4 + i % 2, :], q_stack[0:K_MAX, h, n * P:(n + 1) * P], k_stack[0:K_MAX, h, :],
                           start=True, stop=True).then_inc(a_ps.handle, 1)

                def turn_max(g):
                    max_part_ready.wait(pe, b, g + 1)
                    if g >= 1:
                        max_row_ready.wait(pe, b, g)
                    else:
                        v1_ready.wait(pe, b, 1)
                    if g >= 3:
                        y1_done.wait(pe, b, g - 2)
                    for n in range(NT):
                        last = nc.tensor.transpose(ps[0:2 * HG, 7, n * P // 2:(n + 1) * P // 2].bitcast(BF16),
                                                   max_part[:, g, n, :, :].rearrange("p a h -> p (a h)"), ident_bf[:, :])
                    last.then_inc(max_row_ps.handle, 1)

                def scores(s):
                    g, m = divmod(s, NT)
                    if m == 0:
                        max_loaded[g].wait(pe, b, 32)
                    for pair in range(2):
                        if s >= 1:
                            probs_ready.wait(pe, b, 2 * s - 1 + pair)
                        for j in range(2):
                            h = g * HG + 2 * pair + j
                            last = mm(ps[:, 2 * pair + j, :], k_stack[0:K_EXP, h, m * P:(m + 1) * P], q_stack[0:K_EXP, h, :],
                                      start=True, stop=True)
                        last.then_inc(s_ps.handle, 1)

                def weigh(s):
                    g, m = divmod(s, NT)
                    probs_ready.wait(pe, b, 2 * s + 2)
                    if m == 0 and g >= 1:
                        o_copied.wait(pe, b, g)
                    for hh in range(HG):
                        last = mm(ps[32 * hh:32 * hh + 32, 6, :], v1[:, m, g * HG + hh, :], probs[:, (2 * s + hh // 2) % 4, hh % 2, :],
                                  start=(m == 0), stop=(m == NT - 1))
                    last.then_inc(probs_used.handle, 1)

                def turn_o(g):
                    o_copied.wait(pe, b, g + 1)
                    if g + 2 < G:
                        max_row_ready.wait(pe, b, g + 3)
                    if g >= 1:
                        y1_done.wait(pe, b, g)
                    for n in range(NT):
                        last = nc.tensor.transpose(ps[:, 7, n * P:(n + 1) * P], o_sb[:, g % 2, n * P:(n + 1) * P], ident)
                    last.then_inc(o_tp_ps.handle, 1)

                stacks_loaded.wait(pe, b, stacks_loaded.per_batch)
                qk_ready.wait(pe, b, 2)
                for g in range(2):
                    for hh in range(HG):
                        maxima(g, hh)
                    turn_max(g)
                v1_ready.wait(pe, b, 1)
                for s in range(G * NT):
                    g, m = divmod(s, NT)
                    scores(s)
                    if m == 0 and 1 <= g < G - 1:
                        turn_max(g + 1)
                    if m == 1 and g >= 1:
                        turn_o(g - 1)
                    if g + 2 < G:
                        maxima(g + 2, m)
                    if s:
                        weigh(s - 1)
                weigh(G * NT - 1)
                turn_o(G - 1)
                turn(3)
                project_out(1)

            batch(0)
            with pe.Fori(1, B) as b:
                batch(b)


_INS = ['x', 'mask_BxSx1_fk1', 'mask_BxS_ff1', 'L0_cond_Wq', 'L0_cond_Wk', 'L0_cond_Wv', 'L0_cond_W_emb', 'L0_cond_W_out',
        'L1_cond_q_w', 'L1_cond_k_w', 'L1_cond_v_w', 'L1_cond_emb_w', 'L1_cond_out_w']


def kernel(**inputs):
    import numpy as np
    import concourse.bacc as bacc
    from concourse.bass_utils import run_bass_kernel_spmd

    nc = bacc.Bacc("TRN2", target_bir_lowering=False, num_devices=1)
    arrays = {name: np.ascontiguousarray(inputs[name]) for name in _INS}
    column = lambda *names: [inputs[n].reshape(-1, P).T for n in names]
    pairs = (("ln_w", "norm_w"), ("ln_b", "norm_b"), ("ln2_w", "sb_norm_w"), ("ln2_b", "sb_norm_b"), ("b_emb", "emb_b"))
    arrays["cols"] = np.ascontiguousarray(np.concatenate(
        [c for p0, p1 in pairs for c in column("L0_cond_" + p0, "L1_cond_" + p1)]
        + column("L0_cond_bk", "L1_cond_q_b", "L1_cond_k_b")
        + [inputs["cond_2048"].reshape(B, TE // P, P).transpose(2, 1, 0).reshape(P, -1)], axis=1))
    arrays["mask_cols"] = np.ascontiguousarray(np.concatenate(
        [inputs[n].reshape(B, NT, P).transpose(2, 1, 0) for n in ("mask_BxSx1_fk1", "mask_BxS_ff1")], axis=1))
    arrays["vectors"] = np.concatenate([inputs[n] for n in (
        "L0_cond_bq", "L0_cond_bv", "L1_cond_v_b", "L0_cond_b_out", "L1_cond_out_b")])
    arrays["consts"] = np.concatenate([np.eye(P, dtype=np.float32),
                                       np.kron(np.eye(P // DH0, dtype=np.float32), np.ones((DH0, DH0), np.float32))], axis=1)
    aps = {name: nc.dram_tensor(f"in_{name}", v.shape, mybir.dt.from_np(v.dtype), kind="ExternalInput").ap()
           for name, v in arrays.items()}
    out = nc.dram_tensor("out_0", (B, T, D), F32, kind="ExternalOutput").ap()
    build(nc, aps, out)
    r = run_bass_kernel_spmd(nc, [{f"in_{name}": v for name, v in arrays.items()}], core_ids=[0])
    return r.results[0]["out_0"]
```

```python
from contextlib import ExitStack

import numpy as np

import concourse.bass as bass
from concourse import mybir

P = 128
B, T, D, TE = 4, 512, 256, 512
NT = T // P
KT = D // P
H0, DH0 = 8, 32
H1, DH1 = 16, 16
G, HG = 4, 4
EPS = 1e-5
MASKED = 1.0e6
N_COLS = 46
SPLIT = 6 * DH1
R_MASK = SPLIT
R_MAX = R_MASK + 3
K_MAX = R_MAX
K_EXP = R_MAX + 2
PROBS = 2
PLACES_Q = (slice(0, 3), slice(3, 5), slice(5, 6))
PLACES_K = (slice(1, 6, 2), slice(2, 5, 2), slice(0, 1))

F32 = mybir.dt.float32
BF16 = mybir.dt.bfloat16
ALU = mybir.AluOpType
ACT = mybir.ActivationFunctionType
AX = mybir.AxisListType


class Signal:

    def __init__(self, sem, per_batch):
        self.sem, self.per_batch = sem, per_batch

    def at(self, b, k):
        return b * self.per_batch + k


class Chain:

    def __init__(self, engine, steps, b):
        self.engine, self.steps, self.b, self.k = engine, steps, b, 0

    def __call__(self, instruction):
        self.k += 1
        instruction.then_inc(self.steps.sem, 1)
        self.engine.wait_ge(self.steps.sem, self.steps.at(self.b, self.k))


def build(nc, a, out):
    with ExitStack() as ctx:
        def sb(name, shape, dt=F32):
            return ctx.enter_context(nc.sbuf_tensor(name, shape, dt))

        def sem(name):
            return ctx.enter_context(nc.semaphore(name))

        def counted(name, per_batch):
            return Signal(sem(name), per_batch)

        consts = sb("consts", [P, 2 * P])
        ident = consts[:, 0:P]
        block_diag = consts[:, P:2 * P]
        ident_bf = sb("ident_bf", [P, P], BF16)
        w_qv0 = sb("w_qv0", [P, KT, 2 * D])
        w_k0 = sb("w_k0", [P, KT, D])
        w_out = [sb(f"w_out{i}", [P, KT, D]) for i in range(2)]
        w_q1 = sb("w_q1", [P, KT, D])
        w_k1 = sb("w_k1", [P, KT, D])
        w_v1 = sb("w_v1", [P, KT, D])
        probs = sb("probs", [P, PROBS, HG, T])
        w_emb = probs[:, :, :, :].rearrange("p a b t -> p (a b t)").rearrange("p (i c n) -> p i c n", i=2, c=TE // P)
        cols = sb("cols", [P, N_COLS])
        pair = lambda k: cols[:, k:k + 2 * KT].rearrange("p (i f) -> p i f", f=KT)
        ln_w, ln_b, ln2_w, ln2_b = (pair(2 * KT * k) for k in range(4))
        b_emb = cols[:, 16:24].rearrange("p (i o) -> p i o", o=4)
        bias_col_in = cols[:, 24:30].rearrange("p (i f) -> p i f", f=KT)
        cond = cols[:, 30:46].rearrange("p (c b) -> p c b", b=B)
        ln_b_wide = sb("ln_b_wide", [P, 2, KT, P])
        bias_col = sb("bias_col", [P, 3, KT])
        vec = sb("vec", [P, 5 * D])
        bias_qv0_in = vec[:, 0:2 * D]
        bias_v1_in = vec[:, 2 * D:3 * D]
        bias_out = vec[:, 3 * D:5 * D].rearrange("p (i d) -> p i d", i=2)
        bias_qv0 = sb("bias_qv0", [P, 2 * D])
        bias_v1 = sb("bias_v1", [P, D])
        cond_tanh = sb("cond_tanh", [P, TE // P, B])
        cond_t = sb("cond_t", [P, TE // P, B])
        emb = sb("emb", [P, 2, 4, B])
        emb_s1 = sb("emb_s1", [P, 2, KT, B])
        emb_t = sb("emb_t", [P, 2, KT, B])
        by_batch = sb("by_batch", [P, 16, B])
        film = by_batch[:, 0:8, :].rearrange("p (i c f) b -> p i c f b", i=2, c=2)
        minus_half = sb("minus_half", [P, NT])
        eps_col = sb("eps_col", [P, NT])

        x = sb("x", [P, B, NT, D])
        xn = [sb("xn_in", [P, NT, D]), sb("xn_mid", [P, NT, D])]
        xn_t = sb("xn_t", [P, KT, T])
        stats = [sb(f"stats{i}", [P, NT, 6]) for i in range(2)]
        mean_var = [sb(f"mean_var{i}", [P, NT, 2]) for i in range(2)]
        var_eps = [sb(f"var_eps{i}", [P, NT]) for i in range(2)]
        rstd = [sb(f"rstd{i}", [P, NT]) for i in range(2)]
        spare = sb("spare", [P, 8])
        film_now = sb("film_now", [P, 2 * KT])
        mask_now = sb("mask_now", [P, NT])
        half_h = sb("half_h", [P, KT, T])
        tanh_h = sb("tanh_h", [P, KT, T])
        y = sb("y", [P, NT, D])
        mask1_rows = sb("mask1_rows", [B, T])
        mask1_rest = sb("mask1_rest", [B, 3, T])
        mask1_part = sb("mask1_part", [B, 3, T], BF16)
        qk = sb("qk", [P, KT, 2, T])
        qk_rest = sb("qk_rest", [P, KT, 2, T])
        qk_part = sb("qk_part", [P, 3, KT, 2, T], BF16)
        q_stack = sb("q_stack", [P, H1, T], BF16)
        k_stack = sb("k_stack", [P, H1, T], BF16)
        v_sum = sb("v_sum", [P, NT, D])
        v1 = sb("v1", [P, NT, H1, 32])
        row_max = sb("row_max", [P, G, NT, HG])
        max_rest = sb("max_rest", [P, G, NT, HG])
        max_part = sb("max_part", [P, G, NT, 2, HG], BF16)
        max_row = sb("max_row", [2 * HG, G, T], BF16)
        o_sb = sb("o_sb", [P, 2, T])
        o_rec = sb("o_rec", [P, G, NT, HG])
        def shared(whole, at, shape):
            n = int(np.prod(shape))
            v = whole[:, at:at + n]
            if len(shape) == 1:
                return v
            return v.rearrange("p (a b) -> p a b", b=shape[1])

        room_a = qk[:, :, :, :].rearrange("p f s t -> p (f s t)")
        room_b = qk_rest[:, :, :, :].rearrange("p f s t -> p (f s t)")
        room_c = qk_part[:, :, :, :, :].rearrange("p a f s t -> p (a f s t)").bitcast(F32)
        qv = shared(room_a, 0, [NT, 2 * D])
        k_exp = shared(room_b, 0, [KT, T])
        q_exp = shared(room_b, KT * T, [NT, D])
        q_t = shared(room_c, 0, [KT, T])
        k_tok = shared(room_c, KT * T, [NT, D])
        mask0_wide = shared(room_c, 2 * KT * T, [T])
        att = shared(room_c, 2 * KT * T + T, [KT, P])
        k_negmax = sb("k_negmax", [P, KT])
        k_sum = sb("k_sum", [P, KT])
        k_rec = sb("k_rec", [P, KT])
        q_max = sb("q_max", [P, NT, H0])
        q_sum = sb("q_sum", [P, NT * H0])
        q_rec = sb("q_rec", [P, NT * H0])

        ps = ctx.enter_context(nc.psum_tensor("ps", [P, 8, 512], F32))
        scratch = nc.dram_tensor("scratch", (KT, 2, SPLIT, P // DH1, T), BF16, kind="Internal").ap()
        mask1_scratch = nc.dram_tensor("mask1_scratch", (B, 3, T), BF16, kind="Internal").ap()
        SCORES = 0
        MAXIMA = 3
        OUTPUT = 5
        TURNED = 6
        SIDE = 7

        s_weights, s_consts, s_x = sem("s_weights"), sem("s_consts"), sem("s_x")
        s_tanh_c, s_cond_t = sem("s_tanh_c"), sem("s_cond_t")
        s_emb_ps, s_bias_ps, s_ident_bf, s_wide = sem("s_emb_ps"), sem("s_bias_ps"), sem("s_ident_bf"), sem("s_wide")
        s_setup, s_setup_pool, s_dve0 = sem("s_setup"), sem("s_setup_pool"), sem("s_dve0")
        s_mask_parts, s_mask_kept = sem("s_mask_parts"), sem("s_mask_kept")

        stats_ready = [counted(f"stats_ready{i}", 1) for i in range(4)]
        rstd_ready = [counted(f"rstd_ready{i}", 1) for i in range(4)]
        xn_ready = [counted(f"xn_ready{i}", NT) for i in range(4)]
        tp_ready = [counted(f"tp_ready{i}", KT) for i in range(4)]
        xnt_ready = [counted(f"xnt_ready{i}", KT) for i in range(2)]
        half_ready = [counted(f"half_ready{i}", KT) for i in range(2)]
        tanh_ready = [counted(f"tanh_ready{i}", 1) for i in range(2)]
        silu_ready = [counted(f"silu_ready{i}", 1) for i in range(2)]
        out_ps = [counted(f"out_ps{i}", 2) for i in range(2)]
        plus_ready = [counted(f"plus_ready{i}", 1) for i in range(2)]
        x_ready = [counted(f"x_ready{i}", 2) for i in range(2)]
        mask0_loaded = counted("mask0_loaded", 16)
        k0_ps = counted("k0_ps", KT)
        qv_ps = counted("qv_ps", NT)
        qv_read = counted("qv_read", NT)
        k_max_ready = counted("k_max_ready", KT)
        k_exp_ready = counted("k_exp_ready", KT)
        q_cent_ready = counted("q_cent_ready", 1)
        q_exp_ready = counted("q_exp_ready", 1)
        v0_ready = counted("v0_ready", 1)
        k_tok_ps = counted("k_tok_ps", 1)
        k_tok_ready = counted("k_tok_ready", 1)
        q_t_ps = counted("q_t_ps", 1)
        q_t_ready = counted("q_t_ready", 1)
        att_ps = counted("att_ps", 1)
        att_ready = counted("att_ready", 1)
        y_ps = counted("y_ps", 1)
        y0_ready = counted("y0_ready", 1)
        qk_ps = counted("qk_ps", 2 * KT)
        qk_ready = counted("qk_ready", 2 * KT)
        part0_ready = counted("part0_ready", KT)
        rest_ready = counted("rest_ready", KT)
        part1_ready = counted("part1_ready", KT)
        part2_ready = counted("part2_ready", KT)
        part_kept = [counted(f"part_kept{f}", 6 * 16) for f in range(KT)]
        stack_loaded = [counted(f"stack_loaded{g}", 3 * 16) for g in range(G)]
        v_ps = counted("v_ps", 2)
        v_sum_ready = counted("v_sum_ready", 2)
        v1_ready = counted("v1_ready", 1)
        a_ps = counted("a_ps", G * HG * NT)
        a_read = counted("a_read", G * HG * NT)
        max_part_ready = counted("max_part_ready", G)
        max_row_ps = counted("max_row_ps", G)
        max_row_ready = counted("max_row_ready", G)
        max_loaded = [counted(f"max_loaded{g}", 2 * 16) for g in range(G)]
        s_ps = counted("s_ps", G * NT * HG)
        probs_ready = counted("probs_ready", G * NT * HG)
        probs_used = counted("probs_used", G * NT)
        o_copied = counted("o_copied", G)
        o_tp_ps = counted("o_tp_ps", G)
        y1_done = counted("y1_done", G)
        stored = counted("stored", 16)
        a_done = counted("a_done", 1)
        dve_a = counted("dve_a", 9)
        dve_b = counted("dve_b", 2)
        dve_pre = counted("dve_pre", 1)
        dve_att = counted("dve_att", 2 * G)
        norm_y = counted("norm_y", G)
        dve_post = counted("dve_post", 2)
        mask_now_ready = counted("mask_now_ready", 1)
        pool_norm = [counted(f"pool_norm{i}", 1) for i in range(4)]

        N_WEIGHTS = 10
        N_CONSTS = 5
        SETUP_POOL = 6
        STEPS = G * NT
        XN_PRE, QK_AT, XN_POST, OUT_AT, V_AT = (1, 2), ((3, 4), (7, 8)), (5, 6), (9, 10), (11, 12)
        SECOND_PART = (6, 10)

        block = ctx.enter_context(nc.Block())

        rows = lambda v: v.rearrange("(c p) n -> p c n", p=P)
        tokens_of = lambda b: x[:, bass.ds(b, 1), :, :].rearrange("p a n d -> p (a n) d")

        def first(b):
            return isinstance(b, int) and b == 0

        def layer0(engine, stage_a, both, stage_b):
            stage_a(0)
            with engine.Fori(0, B - 1) as b:
                both(b)
            stage_b(B - 1)

        def maxima_at(pre, att_b, s):
            g, m = divmod(s + 2 + NT, HG)
            if g < G:
                return (att_b, g, m)
            return (pre, g - G, m)

        def rows_turned_at(pre, att_b, s):
            if s % NT != 2:
                return (None, 0)
            return (att_b, s // NT + 1) if s // NT + 1 < G else (pre, 0)

        def layer1(engine, turn):
            turn(0, None, None)
            turn(1, 0, None)
            with engine.Fori(1, B - 1) as b:
                turn(b + 1, b, b - 1)
            turn(None, B - 1, B - 2)
            turn(None, None, B - 1)

        @block.sync
        def _(sp):
            w = lambda dst, src: sp.dma_start(dst, src).then_inc(s_weights, 16)
            c = lambda dst, src: sp.dma_start(dst, src).then_inc(s_consts, 16)
            c(consts[:, :], a["consts"])
            c(cols[:, :], a["cols"])
            c(by_batch[:, 8:16, :], a["mask_cols"])
            w(w_k0[:, :, :], rows(a["L0_cond_Wk"]))
            w(w_qv0[:, :, 0:D], rows(a["L0_cond_Wq"]))
            w(w_qv0[:, :, D:2 * D], rows(a["L0_cond_Wv"]))
            c(mask1_rows[:, :], a["mask_BxS_ff1"])
            c(vec[:, :], a["vectors"].rearrange("(a n) -> a n", a=1).to_broadcast([P, 5 * D]))
            sp.dma_start(x[:, 0, :, :], a["x"][0].rearrange("(n p) d -> p n d", p=P)).then_inc(s_x, 16)
            w(w_q1[:, :, :], rows(a["L1_cond_q_w"]))
            w(w_k1[:, :, :], rows(a["L1_cond_k_w"]))
            w(w_v1[:, :, :], rows(a["L1_cond_v_w"]))
            w(w_emb[:, 0, :, :], rows(a["L0_cond_W_emb"]))
            w(w_emb[:, 1, :, :], rows(a["L1_cond_emb_w"]))
            w(w_out[0][:, :, :], rows(a["L0_cond_W_out"]))
            w(w_out[1][:, :, :], rows(a["L1_cond_out_w"]))
            sp.dma_start(x[:, 1:B, :, :].rearrange("p b n d -> p (b n) d"),
                         a["x"][1:B].rearrange("b (n p) d -> p (b n) d", p=P)).then_inc(s_x, 16)
            sp.wait_ge(s_mask_parts, 1)
            sp.dma_start(mask1_scratch, mask1_part[:, :, :]).then_inc(s_mask_kept, 16)

            def load_mask(b):
                sp.dma_start(mask0_wide, a["mask_BxSx1_fk1"][b].rearrange("t a -> a t").to_broadcast([P, T])
                             ).then_inc(mask0_loaded.sem, 16)

            load_mask(0)
            with sp.Fori(0, B - 1) as b:
                sp.wait_ge(k_max_ready.sem, k_max_ready.at(b, KT))
                load_mask(b + 1)

            def keep(b, f, part):
                ready = (part0_ready, part1_ready, part2_ready)[part]
                for side, places in enumerate((PLACES_Q[part], PLACES_K[part])):
                    to = scratch[f, side].rearrange("(j l) h t -> (l h) j t", j=6)[:, places, :]
                    n = len(range(*places.indices(6)))
                    if side == 0:
                        sp.wait_ge(ready.sem, ready.at(b, f + 1))
                    sp.dma_start(to, qk_part[:, part, f, side, :].unsqueeze(1).to_broadcast([P, n, T])
                                 ).then_inc(part_kept[f].sem, 16)

            def load_stack(b, g):
                f, h = divmod(g * HG, P // DH1)
                sp.wait_ge(part_kept[f].sem, part_kept[f].at(b, 6 * 16))
                for side, stack in enumerate((q_stack, k_stack)):
                    sp.dma_start(stack[0:SPLIT, g * HG:(g + 1) * HG, :], scratch[f, side, :, h:h + HG, :]
                                 ).then_inc(stack_loaded[g].sem, 16)
                sp.dma_start(k_stack[R_MASK:R_MASK + 3, g * HG:(g + 1) * HG, :],
                             mask1_scratch[bass.ds(b, 1)].rearrange("a r t -> r a t").to_broadcast([3, HG, T])
                             ).then_inc(stack_loaded[g].sem, 16)

            def load_max(b, g):
                sp.wait_ge(max_row_ready.sem, max_row_ready.at(b, g + 1))
                for part in range(2):
                    r = R_MAX + part
                    sp.dma_start(q_stack[r:r + 1, g * HG:(g + 1) * HG, :],
                                 max_row[part * HG:(part + 1) * HG, g, :]).then_inc(max_loaded[g].sem, 16)

            def turn(pre, att_b, post):
                if att_b is not None:
                    if not first(att_b):
                        sp.wait_ge(s_ps.sem, s_ps.at(att_b - 1, STEPS * HG))
                    load_stack(att_b, 3)
                    load_max(att_b, 1)
                if pre is not None:
                    keep(pre, 0, 0)
                if att_b is not None:
                    load_max(att_b, 2)
                if pre is not None:
                    keep(pre, 0, 1)
                    keep(pre, 0, 2)
                    if att_b is None:
                        sp.wait_ge(s_mask_kept, 16)
                        sp.wait_ge(s_setup_pool, SETUP_POOL)
                    else:
                        sp.wait_ge(s_ps.sem, s_ps.at(att_b, NT * HG))
                    load_stack(pre, 0)
                    keep(pre, 1, 0)
                    if att_b is not None:
                        sp.wait_ge(s_ps.sem, s_ps.at(att_b, 2 * NT * HG))
                    load_stack(pre, 1)
                if att_b is not None:
                    load_max(att_b, 3)
                if pre is not None:
                    keep(pre, 1, 1)
                    keep(pre, 1, 2)
                if post is not None:
                    sp.wait_ge(x_ready[1].sem, x_ready[1].at(post, 2))
                    sp.dma_start(out[post].rearrange("(n p) d -> p n d", p=P), tokens_of(post)).then_inc(stored.sem, 16)
                if pre is not None:
                    if att_b is not None:
                        sp.wait_ge(s_ps.sem, s_ps.at(att_b, 3 * NT * HG))
                    load_stack(pre, 2)
                    load_max(pre, 0)

            layer1(sp, turn)
            sp.wait_ge(stored.sem, stored.at(B - 1, 16))

        @block.gpsimd
        def _(pool):
            k0 = [0]

            def link(instruction):
                k0[0] += 1
                instruction.then_inc(s_setup_pool, 1)
                pool.wait_ge(s_setup_pool, k0[0])

            link(nc.gpsimd.memset(minus_half[:, :], -0.5))
            link(nc.gpsimd.memset(eps_col[:, :], EPS))
            link(nc.gpsimd.memset(v1[:, :, :, :], 0.0))
            link(nc.gpsimd.memset(v1[:, :, :, DH1:DH1 + 1], 1.0))
            link(nc.gpsimd.memset(q_stack[SPLIT:P, :, :], 1.0))
            link(nc.gpsimd.memset(k_stack[SPLIT:P, :, :], 1.0))
            assert k0[0] == SETUP_POOL
            pool.wait_ge(s_consts, 16 * N_CONSTS)
            link(nc.gpsimd.tensor_scalar(mask1_rest[:, 0, :], mask1_rows[:, :], 1.0, MASKED, ALU.subtract, ALU.mult))
            link(nc.gpsimd.tensor_copy(mask1_part[:, 0, :], mask1_rest[:, 0, :]))
            link(nc.gpsimd.tensor_tensor(mask1_rest[:, 1, :], mask1_rest[:, 0, :], mask1_part[:, 0, :], ALU.subtract))
            link(nc.gpsimd.tensor_copy(mask1_part[:, 1, :], mask1_rest[:, 1, :]))
            link(nc.gpsimd.tensor_tensor(mask1_rest[:, 2, :], mask1_rest[:, 1, :], mask1_part[:, 1, :], ALU.subtract))
            nc.gpsimd.tensor_copy(mask1_part[:, 2, :], mask1_rest[:, 2, :]).then_inc(s_mask_parts, 1)
            pool.wait_ge(s_x, 32)

            def norm(i, b):
                m = i % 2
                pool.wait_ge(stats_ready[i].sem, stats_ready[i].at(b, 1))
                nc.gpsimd.tensor_tensor(var_eps[m][:, :], mean_var[m][:, :, 1], eps_col[:, :], ALU.add).then_inc(pool_norm[i].sem, 1)
                pool.wait_ge(pool_norm[i].sem, pool_norm[i].at(b, 1))
                nc.gpsimd.tensor_tensor(rstd[m][:, :], var_eps[m][:, :], minus_half[:, :], ALU.pow).then_inc(rstd_ready[i].sem, 1)

            def plus_bias(layer, b):
                pool.wait_ge(xn_ready[2 * layer].sem, xn_ready[2 * layer].at(b, NT))
                nc.gpsimd.tensor_tensor(spare[:, 4:5], eps_col[:, 0:1], eps_col[:, 0:1], ALU.add)
                nc.gpsimd.tensor_tensor(tokens_of(b), tokens_of(b), bias_out[:, layer:layer + 1, :].to_broadcast([P, NT, D]),
                                        ALU.add).then_inc(plus_ready[layer].sem, 1)

            def stage_a(b):
                norm(0, b)
                plus_bias(0, b)

            def both(b):
                norm(0, b + 1)
                plus_bias(0, b + 1)
                norm(1, b)

            layer0(pool, stage_a, both, lambda b: norm(1, b))

            def split(b, f):
                pool.wait_ge(part0_ready.sem, part0_ready.at(b, f + 1))
                nc.gpsimd.tensor_tensor(qk_rest[:, f, :, :], qk[:, f, :, :], qk_part[:, 0, f, :, :], ALU.subtract
                                        ).then_inc(rest_ready.sem, 1)
                pool.wait_ge(part1_ready.sem, part1_ready.at(b, f + 1))
                nc.gpsimd.tensor_tensor(qk_part[:, 2, f, :, :], qk_rest[:, f, :, :], qk_part[:, 1, f, :, :], ALU.subtract
                                        ).then_inc(part2_ready.sem, 1)

            def turn(pre, att_b, post):
                if pre is not None:
                    norm(2, pre)
                    plus_bias(1, pre)
                if post is not None:
                    norm(3, post)
                if pre is not None:
                    split(pre, 0)
                    split(pre, 1)

            layer1(pool, turn)

        @block.scalar
        def _(act):
            act.wait_ge(s_consts, 16 * N_CONSTS)
            nc.scalar.activation(cond_tanh[:, :, :], cond, ACT.Tanh, scale=0.5).then_inc(s_tanh_c, 1)

            def take_xn_t(layer, b, f, bank):
                act.wait_ge(tp_ready[2 * layer].sem, tp_ready[2 * layer].at(b, f + 1))
                nc.scalar.copy(xn_t[:, f, :], ps[:, bank, :]).then_inc(xnt_ready[layer].sem, 1)

            def modulate(layer, b, f, bank):
                act.wait_ge(tp_ready[2 * layer + 1].sem, tp_ready[2 * layer + 1].at(b, f + 1))
                nc.scalar.activation(half_h[:, f, :], ps[:, bank, :], ACT.Identity, bias=film_now[:, KT + f:KT + f + 1],
                                     scale=film_now[:, f:f + 1]).then_inc(half_ready[layer].sem, 1)

            def tanh(layer, b):
                act.wait_ge(half_ready[layer].sem, half_ready[layer].at(b, KT))
                nc.scalar.activation(tanh_h[:, :, :], half_h[:, :, :], ACT.Tanh).then_inc(tanh_ready[layer].sem, 1)

            def a_exp_k(b):
                for f in range(KT):
                    act.wait_ge(k_max_ready.sem, k_max_ready.at(b, f + 1))
                    nc.scalar.activation(k_exp[:, f, :], k_exp[:, f, :], ACT.Exp, bias=k_negmax[:, f:f + 1],
                                         accum_out=k_sum[:, f:f + 1]).then_inc(k_exp_ready.sem, 1)

            def a_exp_q(b):
                act.wait_ge(q_cent_ready.sem, q_cent_ready.at(b, 1))
                nc.scalar.activation(q_exp, qv[:, :, 0:D], ACT.Exp).then_inc(q_exp_ready.sem, 1)

            def b_take(b):
                act.wait_ge(k_tok_ps.sem, k_tok_ps.at(b, 1))
                nc.scalar.copy(k_tok, ps[:, 4:6, :]).then_inc(k_tok_ready.sem, 1)
                act.wait_ge(q_t_ps.sem, q_t_ps.at(b, 1))
                nc.scalar.copy(q_t, ps[:, 6:8, :]).then_inc(q_t_ready.sem, 1)

            def take_xn(b):
                for f in range(KT):
                    take_xn_t(0, b, f, f)

            def modulated(b):
                for f in range(KT):
                    modulate(0, b, f, 4 + f)
                tanh(0, b)

            def stage_a(b):
                take_xn(b)
                a_exp_k(b)
                a_exp_q(b)

            def both(b):
                b_take(b)
                take_xn(b + 1)
                a_exp_k(b + 1)
                modulated(b)
                a_exp_q(b + 1)

            def stage_b(b):
                b_take(b)
                modulated(b)

            layer0(act, stage_a, both, stage_b)

            def take_qk(b, f, side):
                act.wait_ge(qk_ps.sem, qk_ps.at(b, 2 * f + side + 1))
                nc.scalar.activation(qk[:, f, side, :], ps[:, SIDE, :], ACT.Identity, bias=bias_col[:, 1 + side, f:f + 1]
                                     ).then_inc(qk_ready.sem, 1)

            def first_part(b, f):
                if not first(b):
                    act.wait_ge(part_kept[f].sem, part_kept[f].at(b - 1, 3 * 16))
                act.wait_ge(qk_ready.sem, qk_ready.at(b, 2 * f + 2))
                nc.scalar.copy(qk_part[:, 0, f, :, :], qk[:, f, :, :]).then_inc(part0_ready.sem, 1)

            def second_part(b, f):
                act.wait_ge(rest_ready.sem, rest_ready.at(b, f + 1))
                nc.scalar.copy(qk_part[:, 1, f, :, :], qk_rest[:, f, :, :]).then_inc(part1_ready.sem, 1)

            def exponential(b, s, hh):
                u = HG * s + hh
                act.wait_ge(s_ps.sem, s_ps.at(b, u + 1))
                if s >= PROBS:
                    act.wait_ge(probs_used.sem, probs_used.at(b, s - PROBS + 1))
                elif not first(b):
                    act.wait_ge(probs_used.sem, probs_used.at(b - 1, STEPS + s - PROBS + 1))
                nc.scalar.activation(probs[:, s % PROBS, hh, :], ps[:, SCORES + u % 3, :], ACT.Exp
                                     ).then_inc(probs_ready.sem, 1)

            def take_o(b, g):
                act.wait_ge(probs_used.sem, probs_used.at(b, NT * (g + 1)))
                if g >= 2:
                    act.wait_ge(o_tp_ps.sem, o_tp_ps.at(b, g - 1))
                elif not first(b):
                    act.wait_ge(o_tp_ps.sem, o_tp_ps.at(b - 1, G + g - 1))
                nc.scalar.copy(o_sb[:, g % 2, :], ps[:, OUTPUT, :]).then_inc(o_copied.sem, 1)

            def read_side(pre, post, s):
                if post is not None and s in XN_POST:
                    modulate(1, post, XN_POST.index(s), SIDE)
                    if s == XN_POST[-1]:
                        tanh(1, post)
                if pre is not None:
                    if s in XN_PRE:
                        take_xn_t(1, pre, XN_PRE.index(s), SIDE)
                    for f in range(KT):
                        if s in QK_AT[f]:
                            take_qk(pre, f, QK_AT[f].index(s))
                            if s == QK_AT[f][-1]:
                                first_part(pre, f)
                        if s == SECOND_PART[f]:
                            second_part(pre, f)

            def turn(pre, att_b, post):
                for s in range(STEPS):
                    for hh in range(HG):
                        if att_b is not None:
                            exponential(att_b, s, hh)
                        if hh == 0:
                            read_side(pre, post, s - 1)
                            if post is not None and s == 0:
                                take_o(post, G - 1)
                        if hh == 2 and att_b is not None and s in (4, 8, 12):
                            take_o(att_b, s // NT - 1)

            layer1(act, turn)

        @block.vector
        def _(dve):
            k0 = [0]

            def link(instruction):
                k0[0] += 1
                instruction.then_inc(s_dve0, 1)
                dve.wait_ge(s_dve0, k0[0])

            dve.wait_ge(s_consts, 16 * N_CONSTS)
            nc.vector.tensor_copy(ident_bf[:, :], ident).then_inc(s_ident_bf, 1)
            nc.vector.tensor_copy(ln_b_wide[:, :, :, :], ln_b[:, :, :].unsqueeze(3).to_broadcast([P, 2, KT, P])
                                  ).then_inc(s_wide, 1)
            dve.wait_ge(s_tanh_c, 1)
            link(nc.vector.scalar_tensor_tensor(cond_t[:, :, :], cond_tanh[:, :, :], 1.0, cond, ALU.add, ALU.mult))
            nc.vector.tensor_scalar(cond_t[:, :, :], cond_t[:, :, :], 0.5, None, ALU.mult).then_inc(s_cond_t, 1)
            dve.wait_ge(s_bias_ps, 1)
            nc.vector.tensor_tensor(bias_col[:, :, :], ps[:, 0, 0:3 * KT].rearrange("p (i f) -> p i f", f=KT),
                                    bias_col_in, ALU.add)
            nc.vector.tensor_tensor(bias_qv0[:, :], ps[:, 1, :], bias_qv0_in, ALU.add)
            nc.vector.tensor_tensor(bias_v1[:, :], ps[:, 2, 0:D], bias_v1_in, ALU.add)
            for f in range(KT):
                for i, wt in ((0, w_k0), (0, w_qv0), (1, w_q1), (1, w_k1), (1, w_v1)):
                    last = nc.vector.tensor_scalar(wt[:, f, :], wt[:, f, :], ln_w[:, i, f:f + 1], None, ALU.mult)
            link(last)
            dve.wait_ge(s_emb_ps, 1)
            link(nc.vector.tensor_tensor(emb[:, :, :, :], ps[:, 4, 0:2 * 4 * B].rearrange("p (i o b) -> p i o b", i=2, o=4),
                                         b_emb[:, :, :].unsqueeze(3).to_broadcast([P, 2, 4, B]), ALU.add))
            link(nc.vector.tensor_scalar(emb_s1[:, :, :, :], emb[:, :, 0:KT, :], 1.0, 0.5, ALU.add, ALU.mult))
            nc.vector.tensor_tensor(film[:, :, 0, :, :], emb_s1[:, :, :, :],
                                    ln2_w[:, :, :].unsqueeze(3).to_broadcast([P, 2, KT, B]), ALU.mult)
            link(nc.vector.tensor_tensor(emb_t[:, :, :, :], emb_s1[:, :, :, :],
                                         ln2_b[:, :, :].unsqueeze(3).to_broadcast([P, 2, KT, B]), ALU.mult))
            for i in range(2):
                last = nc.vector.scalar_tensor_tensor(film[:, i, 1, :, :], emb[:, i, KT:2 * KT, :], 0.5,
                                                      emb_t[:, i, :, :], ALU.mult, ALU.add)
            last.then_inc(s_setup, 1)
            dve.wait_ge(s_setup, 1)
            dve.wait_ge(s_setup_pool, SETUP_POOL)
            dve.wait_ge(s_x, 32)

            def norm_stats(i, b, src, step):
                m = i % 2
                for n in range(NT):
                    last = nc.vector.bn_stats(stats[m][:, n, :], src[:, n, :])
                step(last)
                nc.vector.tensor_copy(spare[:, i:i + 1], stats[m][:, 0, 0:1])
                for n in range(NT):
                    last = nc.vector.bn_aggr(mean_var[m][:, n, :], stats[m][:, n, :])
                last.then_inc(stats_ready[i].sem, 1)

            def norm_apply(i, b, src):
                m = i % 2
                dve.wait_ge(stats_ready[i].sem, stats_ready[i].at(b, 1))
                dve.wait_ge(rstd_ready[i].sem, rstd_ready[i].at(b, 1))
                for n in range(NT):
                    nc.vector.tensor_scalar(xn[m][:, n, :], src[:, n, :], mean_var[m][:, n, 0:1], rstd[m][:, n:n + 1],
                                            ALU.subtract, ALU.mult).then_inc(xn_ready[i].sem, 1)

            def silu(layer, b):
                dve.wait_ge(tanh_ready[layer].sem, tanh_ready[layer].at(b, 1))
                nc.vector.scalar_tensor_tensor(tanh_h[:, :, :], tanh_h[:, :, :], 1.0, half_h[:, :, :],
                                               ALU.add, ALU.mult).then_inc(silu_ready[layer].sem, 1)

            def residual(layer, b, j, bank):
                if j == 0:
                    dve.wait_ge(plus_ready[layer].sem, plus_ready[layer].at(b, 1))
                dve.wait_ge(out_ps[layer].sem, out_ps[layer].at(b, j + 1))
                tiles = x[:, bass.ds(b, 1), 2 * j:2 * j + 2, :].rearrange("p a n d -> p (a n) d")
                nc.vector.tensor_tensor(tiles, ps[:, bank, :].rearrange("p (n d) -> p n d", d=D), tiles,
                                        ALU.add).then_inc(x_ready[layer].sem, 1)

            def this_batch(dst, first, count, b):
                return nc.vector.tensor_copy(dst, by_batch[:, first:first + count, bass.ds(b, 1)].rearrange("p a b -> p (a b)"))

            class A:
                def __init__(self, b):
                    self.b, self.step = b, Chain(dve, dve_a, b)

                def stats(self):
                    norm_stats(0, self.b, tokens_of(self.b), self.step)

                def apply(self):
                    norm_apply(0, self.b, tokens_of(self.b))
                    dve.wait_ge(mask0_loaded.sem, mask0_loaded.at(self.b, 16))
                    self.step(nc.vector.tensor_scalar(mask0_wide, mask0_wide, 1.0, MASKED, ALU.subtract, ALU.mult))

                def keys(self, f):
                    dve.wait_ge(k0_ps.sem, k0_ps.at(self.b, f + 1))
                    self.step(nc.vector.scalar_tensor_tensor(k_exp[:, f, :], ps[:, 2 + f, :], bias_col[:, 0, f:f + 1],
                                                             mask0_wide, ALU.add, ALU.add))
                    nc.vector.tensor_reduce(k_negmax[:, f:f + 1], k_exp[:, f, :], AX.X, ALU.max, negate=True
                                            ).then_inc(k_max_ready.sem, 1)
                    if f == KT - 1:
                        self.step(this_batch(mask_now[:, :], 8, NT, self.b))

                def take_qv(self, n):
                    dve.wait_ge(qv_ps.sem, qv_ps.at(self.b, n + 1))
                    nc.vector.tensor_tensor(qv[:, n, :], ps[:, n, :], bias_qv0[:, :], ALU.add).then_inc(qv_read.sem, 1)

                def centre(self):
                    dve.wait_ge(qv_read.sem, qv_read.at(self.b, NT))
                    q_in = qv[:, :, 0:D].rearrange("p n (h l) -> p n h l", l=DH0)
                    self.step(nc.vector.tensor_reduce(q_max[:, :, :], q_in, AX.X, ALU.max))
                    for n in range(NT):
                        last = nc.vector.tensor_tensor(q_in[:, n], q_in[:, n],
                                                       q_max[:, n, :].unsqueeze(2).to_broadcast([P, H0, DH0]), ALU.subtract)
                    last.then_inc(q_cent_ready.sem, 1)
                    for n in range(NT):
                        last = nc.vector.tensor_scalar(qv[:, n, D:2 * D], qv[:, n, D:2 * D], mask_now[:, n:n + 1], None, ALU.mult)
                    last.then_inc(v0_ready.sem, 1)

                def sums(self):
                    dve.wait_ge(q_exp_ready.sem, q_exp_ready.at(self.b, 1))
                    self.step(nc.vector.tensor_reduce(q_sum[:, :], q_exp.rearrange("p n (h l) -> p (n h) l", l=DH0), AX.X, ALU.add))
                    self.step(nc.vector.reciprocal(q_rec[:, :], q_sum[:, :]))
                    dve.wait_ge(k_exp_ready.sem, k_exp_ready.at(self.b, KT))
                    self.step(nc.vector.reciprocal(k_rec[:, :], k_sum[:, :]))
                    assert self.step.k == dve_a.per_batch, self.step.k
                    this_batch(film_now[:, :], 0, 2 * KT, self.b).then_inc(a_done.sem, 1)

            class Bst:
                def __init__(self, b):
                    self.b, self.step = b, Chain(dve, dve_b, b)

                def attention(self):
                    dve.wait_ge(att_ps.sem, att_ps.at(self.b, 1))
                    for f in range(KT):
                        last = nc.vector.scalar_tensor_tensor(att[:, f, :], ps[:, 4, f * P:(f + 1) * P], k_rec[:, f:f + 1],
                                                              block_diag, ALU.mult, ALU.mult)
                    last.then_inc(att_ready.sem, 1)

                def output(self):
                    dve.wait_ge(y_ps.sem, y_ps.at(self.b, 1))
                    self.step(nc.vector.tensor_tensor(y[:, :, :].rearrange("p n (h l) -> p (n h) l", l=DH0),
                                                      ps[:, 6:8, :].rearrange("p n (h l) -> p (n h) l", l=DH0),
                                                      q_rec[:, :].unsqueeze(2).to_broadcast([P, NT * H0, DH0]), ALU.mult))
                    norm_stats(1, self.b, y, self.step)
                    assert self.step.k == dve_b.per_batch

                def apply(self):
                    norm_apply(1, self.b, y)

                def silu(self):
                    silu(0, self.b)

                def residual(self):
                    for j in range(2):
                        residual(0, self.b, j, 6 + j)

            def stage_a(b):
                st = A(b)
                st.stats()
                st.apply()
                for f in range(KT):
                    st.keys(f)
                for n in range(NT):
                    st.take_qv(n)
                st.centre()
                st.sums()

            def both(b):
                new, old = A(b + 1), Bst(b)
                new.stats()
                old.attention()
                new.apply()
                old.output()
                new.keys(0)
                new.keys(1)
                old.apply()
                for n in range(NT):
                    new.take_qv(n)
                old.silu()
                new.centre()
                old.residual()
                new.sums()

            def stage_b(b):
                st = Bst(b)
                st.attention()
                st.output()
                st.apply()
                st.silu()
                st.residual()

            layer0(dve, stage_a, both, stage_b)

            def maximum(b, g, m, n):
                i = (g * HG + m) * NT + n
                dve.wait_ge(a_ps.sem, a_ps.at(b, i + 1))
                nc.vector.tensor_reduce(row_max[:, g, n, m:m + 1], ps[:, MAXIMA + i % 2, :], AX.X, ALU.max
                                        ).then_inc(a_read.sem, 1)

            def split_max(b, g):
                step = Chain(dve, dve_att, b)
                step.k = 2 * g
                dve.wait_ge(a_read.sem, a_read.at(b, (g + 1) * HG * NT))
                step(nc.vector.tensor_scalar(max_part[:, g, :, 0, :], row_max[:, g, :, :], -1.0, None, ALU.mult))
                step(nc.vector.tensor_tensor(max_rest[:, g, :, :], row_max[:, g, :, :], max_part[:, g, :, 0, :], ALU.add))
                nc.vector.tensor_scalar(max_part[:, g, :, 1, :], max_rest[:, g, :, :], -1.0, None, ALU.mult
                                        ).then_inc(max_part_ready.sem, 1)

            def take_max_row(b, g):
                dve.wait_ge(max_row_ps.sem, max_row_ps.at(b, g + 1))
                if not first(b):
                    dve.wait_ge(max_loaded[g].sem, max_loaded[g].at(b - 1, 32))
                nc.vector.tensor_copy(max_row[:, g, :], ps[0:2 * HG, TURNED, 0:T // 2].bitcast(BF16)
                                      ).then_inc(max_row_ready.sem, 1)

            def normalise(b, g):
                step = Chain(dve, norm_y, b)
                step.k = g
                dve.wait_ge(o_tp_ps.sem, o_tp_ps.at(b, g + 1))
                o = ps[:, TURNED, :].rearrange("p (n h c) -> p n h c", n=NT, h=HG)
                step(nc.vector.reciprocal(o_rec[:, g, :, :], o[:, :, :, DH1]))
                nc.vector.tensor_tensor(
                    y[:, :, g * HG * DH1:(g + 1) * HG * DH1].rearrange("p n (h l) -> p n h l", l=DH1),
                    o[:, :, :, 0:DH1], o_rec[:, g, :, :].unsqueeze(3).to_broadcast([P, NT, HG, DH1]), ALU.mult
                ).then_inc(y1_done.sem, 1)

            def take_v(b, j):
                dve.wait_ge(v_ps.sem, v_ps.at(b, j + 1))
                nc.vector.tensor_tensor(v_sum[:, 2 * j:2 * j + 2, :], ps[:, SIDE, :].rearrange("p (n d) -> p n d", d=D),
                                        bias_v1[:, :].unsqueeze(1).to_broadcast([P, 2, D]), ALU.add
                                        ).then_inc(v_sum_ready.sem, 1)
                if j == 1:
                    this_batch(mask_now[:, :], 12, NT, b).then_inc(mask_now_ready.sem, 1)

            def mask_v(b):
                dve.wait_ge(v_sum_ready.sem, v_sum_ready.at(b, 2))
                dve.wait_ge(mask_now_ready.sem, mask_now_ready.at(b, 1))
                if not first(b):
                    dve.wait_ge(probs_used.sem, probs_used.at(b - 1, STEPS))
                for n in range(NT):
                    last = nc.vector.tensor_scalar(v1[:, n, :, 0:DH1], v_sum[:, n, :].rearrange("p (h l) -> p h l", l=DH1),
                                                   mask_now[:, n:n + 1], None, ALU.mult)
                last.then_inc(v1_ready.sem, 1)

            def read_side(pre, post, s):
                if post is not None and s in OUT_AT:
                    residual(1, post, OUT_AT.index(s), SIDE)
                if pre is not None and s in V_AT:
                    take_v(pre, V_AT.index(s))

            def turn(pre, att_b, post):
                for s in range(STEPS):
                    b, g, m = maxima_at(pre, att_b, s)
                    if b is not None:
                        maximum(b, g, m, 0)
                    read_side(pre, post, s - 1)
                    if b is not None:
                        for n in range(1, NT):
                            maximum(b, g, m, n)
                        if m == HG - 1:
                            split_max(b, g)
                    row_b, row_g = rows_turned_at(pre, att_b, s)
                    if row_b is not None:
                        take_max_row(row_b, row_g)
                    if att_b is not None:
                        if s == 0:
                            mask_v(att_b)
                        if s in (5, 9, 13):
                            normalise(att_b, s // NT - 1)
                    if pre is not None:
                        if s == 0:
                            norm_stats(2, pre, tokens_of(pre), Chain(dve, dve_pre, pre))
                            norm_apply(2, pre, tokens_of(pre))
                    if post is not None:
                        if s == 1:
                            normalise(post, G - 1)
                        if s == 2:
                            dve.wait_ge(y1_done.sem, y1_done.at(post, G))
                            step = Chain(dve, dve_post, post)
                            step(this_batch(film_now[:, :], 2 * KT, 2 * KT, post))
                            norm_stats(3, post, y, step)
                        if s == 3:
                            norm_apply(3, post, y)
                        if s == OUT_AT[0] - 1:
                            silu(1, post)

            layer1(dve, turn)

        @block.tensor
        def _(pe):
            mm = nc.tensor.matmul
            pe.wait_ge(s_weights, 16 * N_WEIGHTS)
            pe.wait_ge(s_wide, 1)
            for i, (layer, wt) in enumerate(((0, w_k0), (1, w_q1), (1, w_k1))):
                for o in range(KT):
                    for f in range(KT):
                        mm(ps[:, 0, i * KT + o:i * KT + o + 1], wt[:, f, o * P:(o + 1) * P], ln_b[:, layer, f:f + 1],
                           start=(f == 0), stop=(f == KT - 1))
            for f in range(KT):
                mm(ps[:, 1, :], ln_b_wide[:, 0, f, :], w_qv0[:, f, :], start=(f == 0), stop=(f == KT - 1))
            for f in range(KT):
                last = mm(ps[:, 2, 0:D], ln_b_wide[:, 1, f, :], w_v1[:, f, :], start=(f == 0), stop=(f == KT - 1))
            last.then_inc(s_bias_ps, 1)
            pe.wait_ge(s_cond_t, 1)
            for i in range(2):
                for o in range(4):
                    for c in range(TE // P):
                        q = (i * 4 + o) * B
                        last = mm(ps[:, 4, q:q + B], w_emb[:, i, c, o * P:(o + 1) * P], cond_t[:, c, :],
                                  start=(c == 0), stop=(c == TE // P - 1))
            last.then_inc(s_emb_ps, 1)
            pe.wait_ge(s_ident_bf, 1)
            pe.wait_ge(s_setup, 1)
            pe.wait_ge(s_setup_pool, SETUP_POOL)

            def turn_xn(i, b, f, bank):
                for n in range(NT):
                    if f == 0:
                        pe.wait_ge(xn_ready[i].sem, xn_ready[i].at(b, n + 1))
                    last = nc.tensor.transpose(ps[:, bank, n * P:(n + 1) * P], xn[i % 2][:, n, f * P:(f + 1) * P], ident)
                last.then_inc(tp_ready[i].sem, 1)

            def turn_half(i, b, f, bank, half):
                for n in (2 * half, 2 * half + 1):
                    if f == 0:
                        pe.wait_ge(xn_ready[i].sem, xn_ready[i].at(b, n + 1))
                    last = nc.tensor.transpose(ps[:, bank, n * P:(n + 1) * P], xn[i % 2][:, n, f * P:(f + 1) * P], ident)
                if half == 1:
                    last.then_inc(tp_ready[i].sem, 1)

            def features(bank, wt, o):
                for f in range(KT):
                    last = mm(ps[:, bank, :], wt[:, f, o * P:(o + 1) * P], xn_t[:, f, :], start=(f == 0), stop=(f == KT - 1))
                return last

            def tokens(out_cols, left, wt, n, width):
                for f in range(KT):
                    last = mm(out_cols, left[:, f, n * P:(n + 1) * P], wt[:, f, 0:width], start=(f == 0), stop=(f == KT - 1))
                return last

            def project_out(layer, b, j, bank):
                pe.wait_ge(silu_ready[layer].sem, silu_ready[layer].at(b, 1))
                for n in (2 * j, 2 * j + 1):
                    last = tokens(ps[:, bank, (n % 2) * D:(n % 2 + 1) * D], tanh_h, w_out[layer], n, D)
                last.then_inc(out_ps[layer].sem, 1)

            def a_turn(b):
                for f in range(KT):
                    turn_xn(0, b, f, f)

            def a_keys(b):
                pe.wait_ge(xnt_ready[0].sem, xnt_ready[0].at(b, KT))
                for o in range(KT):
                    features(2 + o, w_k0, o).then_inc(k0_ps.sem, 1)

            def a_qv(b, tiles):
                for n in tiles:
                    if n >= 2:
                        pe.wait_ge(k_max_ready.sem, k_max_ready.at(b, n - 1))
                    tokens(ps[:, n, :], xn_t, w_qv0, n, 2 * D).then_inc(qv_ps.sem, 1)

            def b_turn(b):
                pe.wait_ge(k_exp_ready.sem, k_exp_ready.at(b, KT))
                pe.wait_ge(q_exp_ready.sem, q_exp_ready.at(b, 1))
                for n in range(NT):
                    for f in range(KT):
                        c = (n % 2) * D + f * P
                        last = nc.tensor.transpose(ps[:, 4 + n // 2, c:c + P], k_exp[:, f, n * P:(n + 1) * P], ident)
                last.then_inc(k_tok_ps.sem, 1)
                pe.wait_ge(a_done.sem, a_done.at(b, 1))
                for f in range(KT):
                    for n in range(NT):
                        last = nc.tensor.transpose(ps[:, 6 + f, n * P:(n + 1) * P], q_exp[:, n, f * P:(f + 1) * P], ident)
                last.then_inc(q_t_ps.sem, 1)

            def b_attention(b):
                pe.wait_ge(k_tok_ready.sem, k_tok_ready.at(b, 1))
                pe.wait_ge(v0_ready.sem, v0_ready.at(b, 1))
                for f in range(KT):
                    for n in range(NT):
                        last = mm(ps[:, 4, f * P:(f + 1) * P], k_tok[:, n, f * P:(f + 1) * P],
                                  qv[:, n, D + f * P:D + (f + 1) * P], start=(n == 0), stop=(n == NT - 1))
                last.then_inc(att_ps.sem, 1)

            def b_output(b):
                pe.wait_ge(att_ready.sem, att_ready.at(b, 1))
                pe.wait_ge(q_t_ready.sem, q_t_ready.at(b, 1))
                for n in range(NT):
                    for f in range(KT):
                        c = (n % 2) * D + f * P
                        last = mm(ps[:, 6 + n // 2, c:c + P], q_t[:, f, n * P:(n + 1) * P], att[:, f, :], start=True, stop=True)
                last.then_inc(y_ps.sem, 1)

            def b_turn_xn(b):
                for f in range(KT):
                    turn_xn(1, b, f, 4 + f)

            def b_project(b):
                for j in range(2):
                    project_out(0, b, j, 6 + j)

            def stage_a(b):
                a_turn(b)
                a_keys(b)
                a_qv(b, range(NT))

            def both(b):
                b_turn(b)
                b_attention(b)
                a_turn(b + 1)
                b_output(b)
                a_keys(b + 1)
                a_qv(b + 1, (0, 1))
                b_turn_xn(b)
                a_qv(b + 1, (2, 3))
                b_project(b)

            def stage_b(b):
                b_turn(b)
                b_attention(b)
                b_output(b)
                b_turn_xn(b)
                b_project(b)

            layer0(pe, stage_a, both, stage_b)

            def maximum(b, g, m, n):
                h = g * HG + m
                if m == 0 and n == 0:
                    pe.wait_ge(stack_loaded[g].sem, stack_loaded[g].at(b, 3 * 16))
                i = h * NT + n
                if i >= 2:
                    pe.wait_ge(a_read.sem, a_read.at(b, i - 1))
                elif not first(b):
                    pe.wait_ge(a_read.sem, a_read.at(b - 1, STEPS * HG + i - 1))
                mm(ps[:, MAXIMA + i % 2, :], q_stack[0:K_MAX, h, n * P:(n + 1) * P], k_stack[0:K_MAX, h, :],
                   start=True, stop=True).then_inc(a_ps.sem, 1)

            def turn_max(b, g):
                pe.wait_ge(max_part_ready.sem, max_part_ready.at(b, g + 1))
                if g >= 2:
                    pe.wait_ge(y1_done.sem, y1_done.at(b, g - 1))
                elif not first(b):
                    pe.wait_ge(y1_done.sem, y1_done.at(b - 1, G - 1 + g))
                elif g == 1:
                    pe.wait_ge(max_row_ready.sem, max_row_ready.at(b, 1))
                for n in range(NT):
                    last = nc.tensor.transpose(ps[0:2 * HG, TURNED, n * P // 2:(n + 1) * P // 2].bitcast(BF16),
                                               max_part[:, g, n, :, :].rearrange("p a h -> p (a h)"), ident_bf[:, :])
                last.then_inc(max_row_ps.sem, 1)

            def scores(b, s, hh):
                g, m = divmod(s, NT)
                if m == 0 and hh == 0:
                    pe.wait_ge(max_loaded[g].sem, max_loaded[g].at(b, 32))
                u = HG * s + hh
                if u >= 3:
                    pe.wait_ge(probs_ready.sem, probs_ready.at(b, u - 2))
                elif not first(b):
                    last_in_bank = max(v for v in range(STEPS * HG) if v % 3 == u)
                    pe.wait_ge(probs_ready.sem, probs_ready.at(b - 1, last_in_bank + 1))
                mm(ps[:, SCORES + u % 3, :], k_stack[0:K_EXP, g * HG + hh, m * P:(m + 1) * P], q_stack[0:K_EXP, g * HG + hh, :],
                   start=True, stop=True).then_inc(s_ps.sem, 1)

            def weigh(b, s):
                g, m = divmod(s, NT)
                if s == 0:
                    pe.wait_ge(v1_ready.sem, v1_ready.at(b, 1))
                if m == 0:
                    if g >= 1:
                        pe.wait_ge(o_copied.sem, o_copied.at(b, g))
                    elif not first(b):
                        pe.wait_ge(o_copied.sem, o_copied.at(b - 1, G))
                for hh in range(HG):
                    pe.wait_ge(probs_ready.sem, probs_ready.at(b, HG * s + hh + 1))
                    last = mm(ps[32 * hh:32 * hh + 32, OUTPUT, :], v1[:, m, g * HG + hh, :], probs[:, s % PROBS, hh, :],
                              start=(m == 0), stop=(m == NT - 1))
                last.then_inc(probs_used.sem, 1)

            def turn_o(b, g):
                pe.wait_ge(o_copied.sem, o_copied.at(b, g + 1))
                if g < G - 1:
                    pe.wait_ge(max_row_ready.sem, max_row_ready.at(b, g + 2))
                elif isinstance(b, int) and b == B - 1:
                    pe.wait_ge(y1_done.sem, y1_done.at(b, G - 1))
                else:
                    pe.wait_ge(max_row_ready.sem, max_row_ready.at(b + 1, 1))
                for n in range(NT):
                    last = nc.tensor.transpose(ps[:, TURNED, n * P:(n + 1) * P], o_sb[:, g % 2, n * P:(n + 1) * P], ident)
                last.then_inc(o_tp_ps.sem, 1)

            def side(pre, post, s, half):
                if pre is not None:
                    if s in XN_PRE:
                        f = XN_PRE.index(s)
                        if half == 0 and f == 1:
                            pe.wait_ge(xnt_ready[1].sem, xnt_ready[1].at(pre, 1))
                        if half == 0 and f == 0 and not first(pre):
                            pe.wait_ge(v_sum_ready.sem, v_sum_ready.at(pre - 1, 2))
                        turn_half(2, pre, f, SIDE, half)
                    if s in QK_AT[0] + QK_AT[1]:
                        k = (QK_AT[0] + QK_AT[1]).index(s)
                        if half == 0:
                            if k == 0:
                                pe.wait_ge(xnt_ready[1].sem, xnt_ready[1].at(pre, 2))
                            else:
                                pe.wait_ge(qk_ready.sem, qk_ready.at(pre, k))
                            if k == 2 and post is not None:
                                pe.wait_ge(half_ready[1].sem, half_ready[1].at(post, 2))
                        wt, o = (w_q1, w_k1)[k % 2], k // 2
                        last = mm(ps[:, SIDE, :], wt[:, half, o * P:(o + 1) * P], xn_t[:, half, :],
                                  start=(half == 0), stop=(half == KT - 1))
                        if half == 1:
                            last.then_inc(qk_ps.sem, 1)
                    if s in V_AT:
                        j = V_AT.index(s)
                        if half == 0 and j == 0:
                            pe.wait_ge(qk_ready.sem, qk_ready.at(pre, 4))
                            if post is not None:
                                pe.wait_ge(x_ready[1].sem, x_ready[1].at(post, 2))
                        if half == 0 and j == 1:
                            pe.wait_ge(v_sum_ready.sem, v_sum_ready.at(pre, 1))
                        last = tokens(ps[:, SIDE, half * D:(half + 1) * D], xn_t, w_v1, 2 * j + half, D)
                        if half == 1:
                            last.then_inc(v_ps.sem, 1)
                if post is not None:
                    if s in XN_POST:
                        f = XN_POST.index(s)
                        if half == 0 and f == 1:
                            pe.wait_ge(half_ready[1].sem, half_ready[1].at(post, 1))
                        if half == 0 and f == 0 and pre is not None:
                            pe.wait_ge(qk_ready.sem, qk_ready.at(pre, 2))
                        turn_half(3, post, f, SIDE, half)
                    if s in OUT_AT:
                        j = OUT_AT.index(s)
                        if half == 0 and j == 0:
                            pe.wait_ge(silu_ready[1].sem, silu_ready[1].at(post, 1))
                            if pre is not None:
                                pe.wait_ge(qk_ready.sem, qk_ready.at(pre, 4))
                        if half == 0 and j == 1:
                            pe.wait_ge(x_ready[1].sem, x_ready[1].at(post, 1))
                        last = tokens(ps[:, SIDE, half * D:(half + 1) * D], tanh_h, w_out[1], 2 * j + half, D)
                        if half == 1:
                            last.then_inc(out_ps[1].sem, 1)

            def turn(pre, att_b, post):
                for s in range(STEPS):
                    b, g, m = maxima_at(pre, att_b, s)
                    for hh in range(HG):
                        if att_b is not None:
                            scores(att_b, s, hh)
                        if b is not None:
                            maximum(b, g, m, hh)
                        if hh == 0:
                            side(pre, post, s - 1, 1)
                            row_b, row_g = rows_turned_at(pre, att_b, s)
                            if row_b is not None:
                                turn_max(row_b, row_g)
                        if hh == 2:
                            if att_b is not None and s >= 1:
                                weigh(att_b, s - 1)
                            if post is not None and s == 0:
                                weigh(post, STEPS - 1)
                        if hh == 3:
                            side(pre, post, s, 0)
                    if att_b is not None and s in (5, 9, 13):
                        turn_o(att_b, s // NT - 1)
                    if post is not None and s == 1:
                        turn_o(post, G - 1)

            layer1(pe, turn)


_INS = ['x', 'mask_BxSx1_fk1', 'mask_BxS_ff1', 'L0_cond_Wq', 'L0_cond_Wk', 'L0_cond_Wv', 'L0_cond_W_emb', 'L0_cond_W_out',
        'L1_cond_q_w', 'L1_cond_k_w', 'L1_cond_v_w', 'L1_cond_emb_w', 'L1_cond_out_w']


def kernel(**inputs):
    import numpy as np
    import concourse.bacc as bacc
    from concourse.bass_utils import run_bass_kernel_spmd

    nc = bacc.Bacc("TRN2", target_bir_lowering=False, num_devices=1)
    arrays = {name: np.ascontiguousarray(inputs[name]) for name in _INS}
    by_feature = lambda v: v.reshape(*v.shape[:-1], KT, P // DH1, DH1).swapaxes(-1, -2).reshape(v.shape)
    for name in ("L1_cond_q_w", "L1_cond_k_w"):
        arrays[name] = np.ascontiguousarray(by_feature(inputs[name]))
    column = lambda *names: [inputs[n].reshape(-1, P).T for n in names]
    pairs = (("ln_w", "norm_w"), ("ln_b", "norm_b"), ("ln2_w", "sb_norm_w"), ("ln2_b", "sb_norm_b"), ("b_emb", "emb_b"))
    arrays["cols"] = np.ascontiguousarray(np.concatenate(
        [c for p0, p1 in pairs for c in column("L0_cond_" + p0, "L1_cond_" + p1)]
        + column("L0_cond_bk") + [by_feature(inputs[n]).reshape(-1, P).T for n in ("L1_cond_q_b", "L1_cond_k_b")]
        + [inputs["cond_2048"].reshape(B, TE // P, P).transpose(2, 1, 0).reshape(P, -1)], axis=1))
    arrays["mask_cols"] = np.ascontiguousarray(np.concatenate(
        [inputs[n].reshape(B, NT, P).transpose(2, 1, 0) for n in ("mask_BxSx1_fk1", "mask_BxS_ff1")], axis=1))
    arrays["vectors"] = np.concatenate([inputs[n] for n in (
        "L0_cond_bq", "L0_cond_bv", "L1_cond_v_b", "L0_cond_b_out", "L1_cond_out_b")])
    arrays["consts"] = np.concatenate([np.eye(P, dtype=np.float32),
                                       np.kron(np.eye(P // DH0, dtype=np.float32), np.ones((DH0, DH0), np.float32))], axis=1)
    aps = {name: nc.dram_tensor(f"in_{name}", v.shape, mybir.dt.from_np(v.dtype), kind="ExternalInput").ap()
           for name, v in arrays.items()}
    out = nc.dram_tensor("out_0", (B, T, D), F32, kind="ExternalOutput").ap()
    build(nc, aps, out)
    r = run_bass_kernel_spmd(nc, [{f"in_{name}": v for name, v in arrays.items()}], core_ids=[0])
    return r.results[0]["out_0"]
```

```python
from contextlib import ExitStack

import concourse.bass as bass
from concourse import mybir

P = 128
B, T, D, TE = 4, 512, 256, 512
NT = T // P
KT = D // P
H0, DH0 = 8, 32
H1, DH1 = 16, 16
G, HG = 4, 4
EPS = 1e-5
MASKED = 1.0e6
N_COLS = 46
SPLIT = 6 * DH1
R_MASK = SPLIT
R_MAX = R_MASK + 3
K_MAX = R_MAX
K_EXP = R_MAX + 2
PROBS = 2
PLACES_Q = (slice(0, 3), slice(3, 5), slice(5, 6))
PLACES_K = (slice(1, 6, 2), slice(2, 5, 2), slice(0, 1))

F32 = mybir.dt.float32
BF16 = mybir.dt.bfloat16
ALU = mybir.AluOpType
ACT = mybir.ActivationFunctionType
AX = mybir.AxisListType


class Signal:

    def __init__(self, sem, per_batch):
        self.sem, self.per_batch = sem, per_batch

    def at(self, b, k):
        return b * self.per_batch + k


class Chain:

    def __init__(self, engine, steps, b):
        self.engine, self.steps, self.b, self.k = engine, steps, b, 0

    def __call__(self, instruction):
        self.k += 1
        instruction.then_inc(self.steps.sem, 1)
        self.engine.wait_ge(self.steps.sem, self.steps.at(self.b, self.k))


def build(nc, a, out):
    with ExitStack() as ctx:
        def sb(name, shape, dt=F32):
            return ctx.enter_context(nc.sbuf_tensor(name, shape, dt))

        def sem(name):
            return ctx.enter_context(nc.semaphore(name))

        def counted(name, per_batch):
            return Signal(sem(name), per_batch)

        consts = sb("consts", [P, 2 * P + B + 2])
        ident = consts[:, 0:P]
        block_diag = consts[:, P:2 * P]
        sum_batches = consts[:, 2 * P:2 * P + B]
        sum_sides = consts[:, 2 * P + B:2 * P + B + 2]
        ident_bf = sb("ident_bf", [P, P], BF16)
        w_qv0 = sb("w_qv0", [P, KT, 2 * D])
        w_k0 = sb("w_k0", [P, KT, D])
        w_out = [sb(f"w_out{i}", [P, KT, D]) for i in range(2)]
        w_q1 = sb("w_q1", [P, KT, D])
        w_k1 = sb("w_k1", [P, KT, D])
        w_v1 = sb("w_v1", [P, KT, D])
        probs = sb("probs", [P, PROBS, HG, T])
        cols = sb("cols", [P, N_COLS])
        pair = lambda k: cols[:, k:k + 2 * KT].rearrange("p (i f) -> p i f", f=KT)
        ln_w, ln_b, ln2_w, ln2_b = (pair(2 * KT * k) for k in range(4))
        b_emb = cols[:, 16:24].rearrange("p (i o) -> p i o", o=4)
        bias_col_in = cols[:, 24:30].rearrange("p (i f) -> p i f", f=KT)
        cond = cols[:, 30:46].rearrange("p (c b) -> p c b", b=B)
        ln_b_wide = sb("ln_b_wide", [P, 2, KT, P])
        bias_col = sb("bias_col", [P, 3, KT])
        vec = sb("vec", [P, 5 * D])
        bias_qv0_in = vec[:, 0:2 * D]
        bias_v1_in = vec[:, 2 * D:3 * D]
        bias_out = vec[:, 3 * D:5 * D].rearrange("p (i d) -> p i d", i=2)
        bias_qv0 = sb("bias_qv0", [P, 2 * D])
        bias_v1 = sb("bias_v1", [P, D])
        cond_tanh = sb("cond_tanh", [P, TE // P, B])
        cond_t = sb("cond_t", [P, TE // P, 32])
        emb = sb("emb", [P, 2, 4, B])
        emb_s1 = sb("emb_s1", [P, 2, KT, B])
        emb_t = sb("emb_t", [P, 2, KT, B])
        by_batch = sb("by_batch", [P, 16, B])
        film = by_batch[:, 0:8, :].rearrange("p (i c f) b -> p i c f b", i=2, c=2)
        minus_half = sb("minus_half", [P, NT])
        eps_col = sb("eps_col", [P, NT])

        x = sb("x", [P, B, NT, D])
        xn = [sb("xn_in", [P, NT, D]), sb("xn_mid", [P, NT, D])]
        xn_t = [sb(f"xn_t{i}", [P, KT, T]) for i in range(2)]
        stats = [sb(f"stats{i}", [P, NT, 6]) for i in range(2)]
        mean_var = [sb(f"mean_var{i}", [P, NT, 2]) for i in range(2)]
        var_eps = [sb(f"var_eps{i}", [P, NT]) for i in range(2)]
        rstd = [sb(f"rstd{i}", [P, NT]) for i in range(2)]
        spare = sb("spare", [P, 8])
        film_now = sb("film_now", [P, 2 * KT])
        mask_now = sb("mask_now", [P, NT])
        half_h = sb("half_h", [P, KT, T])
        tanh_h = sb("tanh_h", [P, KT, T])
        y = sb("y", [P, NT, D])
        mask1_part = sb("mask1_part", [B, 3, T], BF16)
        qk = sb("qk", [P, KT, 2, T])
        qk_rest = sb("qk_rest", [P, KT, 2, T])
        qk_part = sb("qk_part", [P, 3, KT, 2, T], BF16)
        w_emb = [v.rearrange("p (c n) -> p c n", c=TE // P) for v in (
            qk[:, :, :, :].rearrange("p f s t -> p (f s t)"),
            qk_part[:, 0:2, :, :, :].rearrange("p a f s t -> p (a f s t)").bitcast(F32))]
        cond_part, bias_part = tanh_h, half_h[:, 0, 0:D]
        mask1_wide = qk_rest[0:B, :, :, :].rearrange("p f s t -> p (f s) t")
        mask1_rows, mask1_rest = mask1_wide[:, 0, :], mask1_wide[:, 1:4, :]
        q_stack = sb("q_stack", [P, H1, T], BF16)
        k_stack = sb("k_stack", [P, H1, T], BF16)
        v_sum = sb("v_sum", [P, NT, D])
        v1 = sb("v1", [P, NT, H1, 32])
        row_max = sb("row_max", [P, G, NT, HG])
        max_rest = sb("max_rest", [P, G, NT, HG])
        max_part = sb("max_part", [P, G, NT, 2, HG], BF16)
        max_row = sb("max_row", [2 * HG, G, T], BF16)
        o_sb = sb("o_sb", [P, 2, T])
        o_rec = sb("o_rec", [P, G, NT, HG])
        zeros = sb("zeros", [P, T], BF16)
        probs_room = probs[:, :, :, :].rearrange("p a b t -> p (a b t)")
        in_probs = lambda at, n: probs_room[:, at * T:(at + n) * T]
        qv = in_probs(0, 4).rearrange("p (n d) -> p n d", d=2 * D)
        k_exp = in_probs(4, KT).rearrange("p (f t) -> p f t", t=T)
        q_exp = in_probs(6, 2).rearrange("p (n d) -> p n d", d=D)
        q_t = sb("q_t", [P, KT, T])
        k_tok = sb("k_tok", [P, NT, D])
        mask0_wide = sb("mask0_wide", [P, T])
        att = sb("att", [P, KT, P])
        k_negmax = sb("k_negmax", [P, KT])
        k_sum = sb("k_sum", [P, KT])
        k_rec = sb("k_rec", [P, KT])
        q_max = sb("q_max", [P, NT, H0])
        q_sum = sb("q_sum", [P, NT * H0])
        q_rec = sb("q_rec", [P, NT * H0])

        ps = ctx.enter_context(nc.psum_tensor("ps", [P, 8, 512], F32))
        scratch = nc.dram_tensor("scratch", (KT, 2, SPLIT, P // DH1, T), BF16, kind="Internal").ap()
        mask1_scratch = nc.dram_tensor("mask1_scratch", (B, 3, T), BF16, kind="Internal").ap()
        SCORES = 0
        MAXIMA = 3
        OUTPUT = 5
        TURNED = 6
        SIDE = 7

        loads = ("cols", "ident", "x_first", "w_k0_qv0", "vectors", "masks", "w_qkv1", "w_emb", "w_out", "x_rest")
        loaded = {name: sem(f"loaded_{name}") for name in loads}
        s_tanh_c, s_cond_t, s_wide, s_ident_bf = sem("s_tanh_c"), sem("s_cond_t"), sem("s_wide"), sem("s_ident_bf")
        s_bias0_ps, s_weights0, s_bias1_ps, s_setup = sem("s_bias0_ps"), sem("s_weights0"), sem("s_bias1_ps"), sem("s_setup")
        s_setup_pool, s_setup_dve = sem("s_setup_pool"), sem("s_setup_dve")
        s_zeros = sem("s_zeros")
        s_bias1_read = sem("s_bias1_read")
        s_last = sem("s_last")
        s_part_ps, s_part = sem("s_part_ps"), sem("s_part")
        s_mask_parts, s_mask_kept = sem("s_mask_parts"), sem("s_mask_kept")

        stats_ready = [counted(f"stats_ready{i}", 1) for i in range(4)]
        rstd_ready = [counted(f"rstd_ready{i}", 1) for i in range(4)]
        xn_ready = [counted(f"xn_ready{i}", NT) for i in range(4)]
        tp_ready = [counted(f"tp_ready{i}", KT) for i in range(4)]
        xnt_ready = [counted(f"xnt_ready{i}", KT) for i in range(2)]
        half_ready = [counted(f"half_ready{i}", KT) for i in range(2)]
        tanh_ready = [counted(f"tanh_ready{i}", 1) for i in range(2)]
        silu_ready = [counted(f"silu_ready{i}", KT) for i in range(2)]
        out_ps = [counted(f"out_ps{i}", 2) for i in range(2)]
        plus_ready = [counted(f"plus_ready{i}", 1) for i in range(2)]
        x_ready = [counted(f"x_ready{i}", 2) for i in range(2)]
        mask0_loaded = counted("mask0_loaded", 16)
        k0_ps = counted("k0_ps", KT)
        qv_ps = counted("qv_ps", NT)
        qv_read = counted("qv_read", NT)
        k_max_ready = counted("k_max_ready", KT)
        k_exp_ready = counted("k_exp_ready", KT)
        q_cent_ready = counted("q_cent_ready", 2)
        q_exp_ready = counted("q_exp_ready", 2)
        v0_ready = counted("v0_ready", NT)
        k_tok_ps = counted("k_tok_ps", 1)
        k_tok_ready = counted("k_tok_ready", 1)
        q_t_ps = counted("q_t_ps", 1)
        q_t_ready = counted("q_t_ready", 1)
        att_ps = counted("att_ps", 1)
        att_ready = counted("att_ready", 1)
        y_ps = counted("y_ps", 1)
        y0_ready = counted("y0_ready", 1)
        qk_ps = counted("qk_ps", 2 * KT)
        qk_ready = counted("qk_ready", 2 * KT)
        part0_ready = counted("part0_ready", KT)
        rest_ready = counted("rest_ready", KT)
        part1_ready = counted("part1_ready", KT)
        part2_ready = counted("part2_ready", KT)
        part_kept = [counted(f"part_kept{f}", 6 * 16) for f in range(KT)]
        stack_loaded = [counted(f"stack_loaded{g}", 3 * 16) for g in range(G)]
        v_ps = counted("v_ps", 2)
        v_sum_ready = counted("v_sum_ready", 2)
        v1_ready = counted("v1_ready", NT)
        a_ps = counted("a_ps", G * HG * NT)
        a_read = counted("a_read", G * HG * NT)
        max_part_ready = counted("max_part_ready", G)
        max_row_ps = counted("max_row_ps", G)
        max_row_ready = counted("max_row_ready", G)
        max_loaded = [counted(f"max_loaded{g}", 2 * 16) for g in range(G)]
        s_ps = counted("s_ps", G * NT * HG)
        probs_ready = counted("probs_ready", G * NT * HG)
        probs_used = counted("probs_used", G * NT)
        o_copied = counted("o_copied", G)
        o_tp_ps = counted("o_tp_ps", G)
        y1_done = counted("y1_done", G)
        stored = counted("stored", 16)
        dve_a = counted("dve_a", 7)
        dve_b = counted("dve_b", 5)
        dve_pre = counted("dve_pre", 1)
        dve_att = counted("dve_att", 2 * G)
        norm_y = counted("norm_y", G)
        dve_post = counted("dve_post", 2)
        mask_now_ready = counted("mask_now_ready", 1)
        pool_norm = [counted(f"pool_norm{i}", 1) for i in range(4)]

        SETUP_POOL = 6
        STEPS = G * NT
        tail = {name: sem(f"tail_{name}") for name in ("sum", "stats", "var", "rstd", "xn", "tp", "half", "tanh", "silu", "out", "x")}
        half_of = lambda j: slice(j * T // 2, (j + 1) * T // 2)
        OUT_BANKS = (4, SIDE)

        WARM_START, WARM_NORM, WARM_PARTS, WARM_EARLY, WARM_LAST_NORM, WARM_LAST_TANH = 16, 4, 6, 5, 16, 8

        XN_POST, OUT_AT = (5, 6), (9, 10)
        PRE_AT = {1: ("xn", 0), 2: ("xn", 1), 3: ("qk", 0), 4: ("qk", 1), 7: ("qk", 2), 8: ("qk", 3), 11: ("v", 0), 12: ("v", 1)}
        SECOND_PART = {6: 0, 10: 1}
        FIRST_PRE_AT = {1: ("qk", 2), 2: ("qk", 3), 3: ("v", 0), 4: ("v", 1)}
        FIRST_SECOND_PART = {4: 1}
        FIRST_MAXIMA = 4

        block = ctx.enter_context(nc.Block())

        rows = lambda v: v.rearrange("(c p) n -> p c n", p=P)
        tokens_of = lambda b: x[:, bass.ds(b, 1), :, :].rearrange("p a n d -> p (a n) d")

        def first(b):
            return isinstance(b, int) and b == 0

        TURN_AT, ATT_AT, Y_AT, NORM_AT, XN_AT, SILU_AT, LAST_AT = 0, 1, 2, 3, 4, 5, 6

        TWO_ONES = 1.0 + 0x3F80 / 2 ** 23
        EARLY_BANK = 5

        def layer0(engine, stage_a, both):
            stage_a(0)
            with engine.Fori(0, B - 2) as b:
                both(b)
            both(B - 2, early=True)

        def maxima_at(pre, att_b, s):
            if att_b is None:
                if FIRST_MAXIMA <= s < FIRST_MAXIMA + HG + 2:
                    return (pre, *divmod(s - FIRST_MAXIMA, HG))
                return (None, 0, 0)
            g, m = divmod(s + 2 + NT, HG)
            if g < G:
                return (att_b, g, m)
            return (pre, g - G, m)

        def piece(pre, s):
            return (FIRST_PRE_AT if first(pre) else PRE_AT).get(s, (None, 0))

        def rows_turned_at(pre, att_b, s):
            if att_b is None:
                return (pre if s == FIRST_MAXIMA + HG else None, 0)
            if s % NT != 2:
                return (None, 0)
            return (att_b, s // NT + 1) if s // NT + 1 < G else (pre, 0)

        def layer1(engine, turn, last_b, last_post):
            turn(0, None, None, last_b)
            turn(1, 0, None)
            with engine.Fori(1, B - 1) as b:
                turn(b + 1, b, b - 1)
            turn(None, B - 1, B - 2)
            last_post()

        @block.sync
        def _(sp):
            def load(name, dst, src):
                sp.dma_start(dst, src).then_inc(loaded[name], 16)

            def load_mask(b):
                sp.dma_start(mask0_wide[:, :], a["mask_BxSx1_fk1"][b].rearrange("t a -> a t").to_broadcast([P, T])
                             ).then_inc(mask0_loaded.sem, 16)

            load("cols", cols[:, :], a["cols"])
            load("x_first", x[:, 0, :, :], a["x"][0].rearrange("(n p) d -> p n d", p=P))
            load("w_k0_qv0", w_k0[:, :, :], rows(a["L0_cond_Wk"]))
            load("w_k0_qv0", w_qv0[:, :, 0:D], rows(a["L0_cond_Wq"]))
            load("w_k0_qv0", w_qv0[:, :, D:2 * D], rows(a["L0_cond_Wv"]))
            load("ident", consts[:, :], a["consts"])
            load("vectors", vec[:, :], a["vectors"].rearrange("(a n) -> a n", a=1).to_broadcast([P, 5 * D]))
            load_mask(0)
            load("masks", by_batch[:, 8:16, :], a["mask_cols"])
            load("masks", mask1_rows, a["mask_BxS_ff1"])
            load("w_emb", w_emb[0], rows(a["L0_cond_W_emb"]))
            load("w_emb", w_emb[1], rows(a["L1_cond_emb_w"]))
            load("w_qkv1", w_q1[:, :, :], rows(a["L1_cond_q_w"]))
            load("w_qkv1", w_k1[:, :, :], rows(a["L1_cond_k_w"]))
            load("w_qkv1", w_v1[:, :, :], rows(a["L1_cond_v_w"]))
            load("x_rest", x[:, 1:B, :, :].rearrange("p b n d -> p (b n) d"),
                 a["x"][1:B].rearrange("b (n p) d -> p (b n) d", p=P))
            load("w_out", w_out[0][:, :, :], rows(a["L0_cond_W_out"]))
            load("w_out", w_out[1][:, :, :], rows(a["L1_cond_out_w"]))
            sp.wait_ge(s_mask_parts, 1)
            sp.dma_start(mask1_scratch, mask1_part[:, :, :]).then_inc(s_mask_kept, 16)
            with sp.Fori(0, B - 1) as b:
                sp.wait_ge(k_max_ready.sem, k_max_ready.at(b, KT))
                load_mask(b + 1)

            def keep(b, f, part):
                ready = (part0_ready, part1_ready, part2_ready)[part]
                for side, places in enumerate((PLACES_Q[part], PLACES_K[part])):
                    to = scratch[f, side].rearrange("(j l) h t -> (l h) j t", j=6)[:, places, :]
                    n = len(range(*places.indices(6)))
                    if side == 0:
                        sp.wait_ge(ready.sem, ready.at(b, f + 1))
                    sp.dma_start(to, qk_part[:, part, f, side, :].unsqueeze(1).to_broadcast([P, n, T])
                                 ).then_inc(part_kept[f].sem, 16)

            def load_stack(b, g):
                f, h = divmod(g * HG, P // DH1)
                sp.wait_ge(part_kept[f].sem, part_kept[f].at(b, 6 * 16))
                for side, stack in enumerate((q_stack, k_stack)):
                    sp.dma_start(stack[0:SPLIT, g * HG:(g + 1) * HG, :], scratch[f, side, :, h:h + HG, :]
                                 ).then_inc(stack_loaded[g].sem, 16)
                sp.dma_start(k_stack[R_MASK:R_MASK + 3, g * HG:(g + 1) * HG, :],
                             mask1_scratch[bass.ds(b, 1)].rearrange("a r t -> r a t").to_broadcast([3, HG, T])
                             ).then_inc(stack_loaded[g].sem, 16)

            def load_max(b, g):
                sp.wait_ge(max_row_ready.sem, max_row_ready.at(b, g + 1))
                for part in range(2):
                    r = R_MAX + part
                    sp.dma_start(q_stack[r:r + 1, g * HG:(g + 1) * HG, :],
                                 max_row[part * HG:(part + 1) * HG, g, :]).then_inc(max_loaded[g].sem, 16)

            def turn(pre, att_b, post, beside=lambda s: None):
                if att_b is not None:
                    if not first(att_b):
                        sp.wait_ge(s_ps.sem, s_ps.at(att_b - 1, STEPS * HG))
                    load_stack(att_b, 3)
                    load_max(att_b, 1)
                if pre is not None:
                    keep(pre, 0, 0)
                if att_b is not None:
                    load_max(att_b, 2)
                if pre is not None:
                    keep(pre, 0, 1)
                    keep(pre, 0, 2)
                    if att_b is None:
                        sp.wait_ge(s_mask_kept, 16)
                        sp.wait_ge(s_setup_pool, SETUP_POOL)
                    else:
                        sp.wait_ge(s_ps.sem, s_ps.at(att_b, NT * HG))
                    load_stack(pre, 0)
                    keep(pre, 1, 0)
                    if att_b is not None:
                        sp.wait_ge(s_ps.sem, s_ps.at(att_b, 2 * NT * HG))
                    load_stack(pre, 1)
                if att_b is not None:
                    load_max(att_b, 3)
                if pre is not None:
                    keep(pre, 1, 1)
                    keep(pre, 1, 2)
                if post is not None:
                    sp.wait_ge(x_ready[1].sem, x_ready[1].at(post, 2))
                    sp.dma_start(out[post].rearrange("(n p) d -> p n d", p=P), tokens_of(post)).then_inc(stored.sem, 16)
                if pre is not None:
                    if att_b is not None:
                        sp.wait_ge(s_ps.sem, s_ps.at(att_b, 3 * NT * HG))
                    load_stack(pre, 2)
                    load_max(pre, 0)

            def last_post():
                for j in range(2):
                    sp.wait_ge(tail["x"], j + 1)
                    sp.dma_start(out[B - 1, j * T // 2:(j + 1) * T // 2].rearrange("(n p) d -> p n d", p=P),
                                 x[:, B - 1, 2 * j:2 * j + 2, :]).then_inc(s_last, 16)

            layer1(sp, turn, lambda s: None, last_post)
            sp.wait_ge(stored.sem, stored.at(B - 2, 16))
            sp.wait_ge(s_last, 2 * 16)

        @block.gpsimd
        def _(pool):
            k0 = [0]

            def link(instruction):
                k0[0] += 1
                instruction.then_inc(s_setup_pool, 1)
                pool.wait_ge(s_setup_pool, k0[0])

            link(nc.gpsimd.memset(minus_half[:, :], -0.5))
            link(nc.gpsimd.memset(eps_col[:, :], EPS))

            def clear():
                for stack in (q_stack, k_stack):
                    link(nc.gpsimd.memset(stack[SPLIT:P, :, :].rearrange("p h t -> p (h t)").bitcast(F32), TWO_ONES))
                link(nc.gpsimd.memset(v1[:, :, :, :], 0.0))
                link(nc.gpsimd.memset(v1[:, :, :, DH1:DH1 + 1], 1.0))
                assert k0[0] == SETUP_POOL
                pool.wait_ge(loaded["masks"], 2 * 16)
                link(nc.gpsimd.tensor_scalar(mask1_rest[:, 0, :], mask1_rows, 1.0, MASKED, ALU.subtract, ALU.mult))
                link(nc.gpsimd.tensor_copy(mask1_part[:, 0, :], mask1_rest[:, 0, :]))
                link(nc.gpsimd.tensor_tensor(mask1_rest[:, 1, :], mask1_rest[:, 0, :], mask1_part[:, 0, :], ALU.subtract))
                link(nc.gpsimd.tensor_copy(mask1_part[:, 1, :], mask1_rest[:, 1, :]))
                link(nc.gpsimd.tensor_tensor(mask1_rest[:, 2, :], mask1_rest[:, 1, :], mask1_part[:, 1, :], ALU.subtract))
                nc.gpsimd.tensor_copy(mask1_part[:, 2, :], mask1_rest[:, 2, :]).then_inc(s_mask_parts, 1)

            def norm(i, b):
                m = i % 2
                pool.wait_ge(stats_ready[i].sem, stats_ready[i].at(b, 1))
                nc.gpsimd.tensor_tensor(var_eps[m][:, :], mean_var[m][:, :, 1], eps_col[:, :], ALU.add).then_inc(pool_norm[i].sem, 1)
                pool.wait_ge(pool_norm[i].sem, pool_norm[i].at(b, 1))
                nc.gpsimd.tensor_tensor(rstd[m][:, :], var_eps[m][:, :], minus_half[:, :], ALU.pow).then_inc(rstd_ready[i].sem, 1)

            def plus_bias(layer, b):
                pool.wait_ge(xn_ready[2 * layer].sem, xn_ready[2 * layer].at(b, NT))
                nc.gpsimd.tensor_tensor(spare[:, 4:5], eps_col[:, 0:1], eps_col[:, 0:1], ALU.add)
                nc.gpsimd.tensor_tensor(tokens_of(b), tokens_of(b), bias_out[:, layer:layer + 1, :].to_broadcast([P, NT, D]),
                                        ALU.add).then_inc(plus_ready[layer].sem, 1)

            def split(b, f):
                pool.wait_ge(part0_ready.sem, part0_ready.at(b, f + 1))
                nc.gpsimd.tensor_tensor(qk_rest[:, f, :, :], qk[:, f, :, :], qk_part[:, 0, f, :, :], ALU.subtract
                                        ).then_inc(rest_ready.sem, 1)
                pool.wait_ge(part1_ready.sem, part1_ready.at(b, f + 1))
                nc.gpsimd.tensor_tensor(qk_part[:, 2, f, :, :], qk_rest[:, f, :, :], qk_part[:, 1, f, :, :], ALU.subtract
                                        ).then_inc(part2_ready.sem, 1)

            def stage_a(b):
                norm(0, b)
                pool.wait_ge(loaded["vectors"], 16)
                plus_bias(0, b)
                pool.wait_ge(plus_ready[0].sem, plus_ready[0].at(b, 1))
                clear()
                pool.wait_ge(loaded["x_rest"], 16)

            def both(b, early=False):
                norm(0, b + 1)
                plus_bias(0, b + 1)
                if early:
                    norm(2, 0)
                norm(1, b)
                if early:
                    split(0, 0)

            layer0(pool, stage_a, both)

            def last_b(s):
                if s == Y_AT:
                    norm(1, B - 1)

            def turn(pre, att_b, post, beside=lambda s: None):
                if pre is not None and not first(pre):
                    norm(2, pre)
                for s in range(STEPS):
                    beside(s)
                if post is not None:
                    norm(3, post)
                if pre is not None:
                    if not first(pre):
                        split(pre, 0)
                    plus_bias(1, pre)
                    split(pre, 1)

            def last_post():
                for j in range(2):
                    two = slice(2 * j, 2 * j + 2)
                    pool.wait_ge(tail["stats"], j + 1)
                    nc.gpsimd.tensor_tensor(var_eps[1][:, two], mean_var[1][:, two, 1], eps_col[:, two], ALU.add).then_inc(tail["var"], 1)
                    pool.wait_ge(tail["var"], j + 1)
                    nc.gpsimd.tensor_tensor(rstd[1][:, two], var_eps[1][:, two], minus_half[:, two], ALU.pow).then_inc(tail["rstd"], 1)
                    pool.wait_ge(tail["rstd"], j + 1)

            layer1(pool, turn, last_b, last_post)

        @block.scalar
        def _(act):
            act.wait_ge(loaded["cols"], 16)
            nc.scalar.activation(cond_tanh[:, :, :], cond, ACT.Tanh, scale=0.5).then_inc(s_tanh_c, 1)

            def take_xn_t(layer, b, f, bank):
                act.wait_ge(tp_ready[2 * layer].sem, tp_ready[2 * layer].at(b, f + 1))
                nc.scalar.copy(xn_t[layer][:, f, :], ps[:, bank, :]).then_inc(xnt_ready[layer].sem, 1)

            def modulate(layer, b, f, bank):
                act.wait_ge(tp_ready[2 * layer + 1].sem, tp_ready[2 * layer + 1].at(b, f + 1))
                nc.scalar.activation(half_h[:, f, :], ps[:, bank, :], ACT.Identity, bias=film_now[:, KT + f:KT + f + 1],
                                     scale=film_now[:, f:f + 1]).then_inc(half_ready[layer].sem, 1)

            def tanh(layer, b):
                act.wait_ge(half_ready[layer].sem, half_ready[layer].at(b, KT))
                nc.scalar.activation(tanh_h[:, :, :], half_h[:, :, :], ACT.Tanh).then_inc(tanh_ready[layer].sem, 1)

            def take_qk(b, f, side, bank):
                act.wait_ge(qk_ps.sem, qk_ps.at(b, 2 * f + side + 1))
                nc.scalar.activation(qk[:, f, side, :], ps[:, bank, :], ACT.Identity, bias=bias_col[:, 1 + side, f:f + 1]
                                     ).then_inc(qk_ready.sem, 1)

            def first_part(b, f):
                if not first(b):
                    act.wait_ge(part_kept[f].sem, part_kept[f].at(b - 1, 3 * 16))
                act.wait_ge(qk_ready.sem, qk_ready.at(b, 2 * f + 2))
                nc.scalar.copy(qk_part[:, 0, f, :, :], qk[:, f, :, :]).then_inc(part0_ready.sem, 1)

            def second_part(b, f):
                act.wait_ge(rest_ready.sem, rest_ready.at(b, f + 1))
                nc.scalar.copy(qk_part[:, 1, f, :, :], qk_rest[:, f, :, :]).then_inc(part1_ready.sem, 1)

            def a_exp_k(b):
                for f in range(KT):
                    act.wait_ge(k_max_ready.sem, k_max_ready.at(b, f + 1))
                    nc.scalar.activation(k_exp[:, f, :], k_exp[:, f, :], ACT.Exp, bias=k_negmax[:, f:f + 1],
                                         accum_out=k_sum[:, f:f + 1]).then_inc(k_exp_ready.sem, 1)

            def a_half(b, j):
                for n in (2 * j, 2 * j + 1):
                    act.wait_ge(qv_read.sem, qv_read.at(b, n + 1))
                    nc.scalar.activation(qv[:, n, D:2 * D], qv[:, n, D:2 * D], ACT.Copy, scale=mask_now[:, n:n + 1]
                                         ).then_inc(v0_ready.sem, 1)
                act.wait_ge(q_cent_ready.sem, q_cent_ready.at(b, j + 1))
                nc.scalar.activation(q_exp[:, 2 * j:2 * j + 2, :], qv[:, 2 * j:2 * j + 2, 0:D], ACT.Exp
                                     ).then_inc(q_exp_ready.sem, 1)

            def b_take(b, bank, q_bank):
                act.wait_ge(k_tok_ps.sem, k_tok_ps.at(b, 1))
                nc.scalar.copy(k_tok[:, :, :], ps[:, bank:bank + 2, :]).then_inc(k_tok_ready.sem, 1)
                act.wait_ge(q_t_ps.sem, q_t_ps.at(b, 1))
                nc.scalar.copy(q_t[:, :, :], ps[:, q_bank:q_bank + 2, :]).then_inc(q_t_ready.sem, 1)

            def take_xn(b):
                for f in range(KT):
                    take_xn_t(0, b, f, f)

            def modulated(b, banks):
                for f in range(KT):
                    modulate(0, b, f, banks[f])
                tanh(0, b)

            def stage_a(b):
                take_xn(b)
                a_exp_k(b)
                for i in range(2):
                    act.wait_ge(s_part_ps, i + 1)
                    nc.scalar.copy(cond_part[:, i, :], ps[:, 6 + i, :]).then_inc(s_part, 1)
                act.wait_ge(s_part_ps, 3)
                nc.scalar.copy(bias_part, ps[:, 5, 0:D]).then_inc(s_part, 1)
                for j in range(2):
                    a_half(b, j)

            def both(b, early=False):
                b_take(b, 4, 2)
                take_xn(b + 1)
                a_exp_k(b + 1)
                if early:
                    take_xn_t(1, 0, 0, EARLY_BANK)
                modulated(b, (4, 6) if early else (4, 5))
                if early:
                    take_xn_t(1, 0, 1, EARLY_BANK)
                    take_qk(0, 0, 0, EARLY_BANK)
                a_half(b + 1, 0)
                if early:
                    take_qk(0, 0, 1, EARLY_BANK)
                    first_part(0, 0)
                a_half(b + 1, 1)
                if early:
                    second_part(0, 0)

            layer0(act, stage_a, both)
            act.wait_ge(s_setup_pool, SETUP_POOL)

            def last_b(s):
                if s == TURN_AT:
                    b_take(B - 1, 0, 2)
                if s == XN_AT:
                    modulated(B - 1, (0, 1))

            def exponential(b, s, hh):
                u = HG * s + hh
                act.wait_ge(s_ps.sem, s_ps.at(b, u + 1))
                if s >= PROBS:
                    act.wait_ge(probs_used.sem, probs_used.at(b, s - PROBS + 1))
                elif not first(b):
                    act.wait_ge(probs_used.sem, probs_used.at(b - 1, STEPS + s - PROBS + 1))
                nc.scalar.activation(probs[:, s % PROBS, hh, :], ps[:, SCORES + u % 3, :], ACT.Exp
                                     ).then_inc(probs_ready.sem, 1)

            def take_max_row(b, g):
                act.wait_ge(max_row_ps.sem, max_row_ps.at(b, g + 1))
                if not first(b):
                    act.wait_ge(max_loaded[g].sem, max_loaded[g].at(b - 1, 32))
                nc.scalar.copy(max_row[:, g, :], ps[0:2 * HG, TURNED, 0:T // 2].bitcast(BF16)
                                      ).then_inc(max_row_ready.sem, 1)

            def mask_v(b, n):
                if n == 0:
                    act.wait_ge(v_sum_ready.sem, v_sum_ready.at(b, 2))
                    act.wait_ge(mask_now_ready.sem, mask_now_ready.at(b, 1))
                if not first(b):
                    act.wait_ge(probs_used.sem, probs_used.at(b - 1, STEPS - NT + n + 1))
                nc.scalar.activation(v1[:, n, :, 0:DH1], v_sum[:, n, :].rearrange("p (h l) -> p h l", l=DH1), ACT.Copy,
                                     scale=mask_now[:, n:n + 1]).then_inc(v1_ready.sem, 1)

            def take_o(b, g):
                act.wait_ge(probs_used.sem, probs_used.at(b, NT * (g + 1)))
                if g >= 2:
                    act.wait_ge(o_tp_ps.sem, o_tp_ps.at(b, g - 1))
                elif not first(b):
                    act.wait_ge(o_tp_ps.sem, o_tp_ps.at(b - 1, G + g - 1))
                nc.scalar.copy(o_sb[:, g % 2, :], ps[:, OUTPUT, :]).then_inc(o_copied.sem, 1)

            def read_side(pre, post, s):
                if post is not None and s in XN_POST:
                    modulate(1, post, XN_POST.index(s), SIDE)
                    if s == XN_POST[-1]:
                        tanh(1, post)
                if pre is not None:
                    what, k = piece(pre, s)
                    if what == "xn":
                        take_xn_t(1, pre, k, SIDE)
                    if what == "qk":
                        take_qk(pre, k // 2, k % 2, SIDE)
                        if k % 2 == 1:
                            first_part(pre, k // 2)
                    seconds = FIRST_SECOND_PART if first(pre) else SECOND_PART
                    if s in seconds:
                        second_part(pre, seconds[s])

            def turn(pre, att_b, post, beside=lambda s: None):
                for s in range(STEPS):
                    beside(s)
                    for hh in range(HG):
                        if att_b is not None:
                            exponential(att_b, s, hh)
                        if hh == 0:
                            read_side(pre, post, s - 1)
                        if hh == 1 and att_b is not None and s in (4, 8, 12):
                            take_o(att_b, s // NT - 1)
                        if hh == 2 and post is not None and s == 0:
                            take_o(post, G - 1)
                        row_b, row_g = rows_turned_at(pre, att_b, s)
                        if hh == 2 and row_b is not None:
                            take_max_row(row_b, row_g)
                        if hh == 2 and pre is not None and s >= STEPS - 2:
                            mask_v(pre, s - (STEPS - 2))
                        if hh == 3 and att_b is not None and s <= 1:
                            mask_v(att_b, 2 + s)

            def last_post():
                take_o(B - 1, G - 1)
                for j in range(2):
                    for f in range(KT):
                        act.wait_ge(tail["tp"], KT * j + f + 1)
                        nc.scalar.activation(half_h[:, f, half_of(j)], ps[:, KT * j + f, 0:T // 2], ACT.Identity,
                                             bias=film_now[:, KT + f:KT + f + 1], scale=film_now[:, f:f + 1]
                                             ).then_inc(tail["half"], 1)
                    act.wait_ge(tail["half"], KT * (j + 1))
                    nc.scalar.activation(tanh_h[:, :, half_of(j)], half_h[:, :, half_of(j)], ACT.Tanh).then_inc(tail["tanh"], 1)

            layer1(act, turn, last_b, last_post)

        @block.vector
        def _(dve):
            k0 = [0]

            def link(instruction):
                k0[0] += 1
                instruction.then_inc(s_setup_dve, 1)
                dve.wait_ge(s_setup_dve, k0[0])

            nc.vector.memset(zeros[:, :], 0.0).then_inc(s_zeros, 1)

            def weights0():
                dve.wait_ge(loaded["cols"], 16)
                nc.vector.tensor_copy(ln_b_wide[:, :, :, :], ln_b[:, :, :].unsqueeze(3).to_broadcast([P, 2, KT, P])
                                      ).then_inc(s_wide, 1)
                dve.wait_ge(s_tanh_c, 1)
                link(nc.vector.memset(cond_t[:, :, :], 0.0))
                now = cond_t[:, :, 0:B]
                link(nc.vector.scalar_tensor_tensor(now, cond_tanh[:, :, :], 1.0, cond, ALU.add, ALU.mult))
                nc.vector.tensor_scalar(now, now, 0.5, None, ALU.mult).then_inc(s_cond_t, 1)

            def gains(layer, weights):
                for f in range(KT):
                    for wt in weights:
                        last = nc.vector.tensor_scalar(wt[:, f, :], wt[:, f, :], ln_w[:, layer, f:f + 1], None, ALU.mult)
                return last

            def biases0():
                dve.wait_ge(s_bias0_ps, 1)
                gains(0, (w_k0, w_qv0)).then_inc(s_weights0, 1)
                nc.vector.tensor_tensor(bias_col[:, 0, :], ps[:, 4, 0:KT], bias_col_in[:, 0, :], ALU.add)
                dve.wait_ge(loaded["vectors"], 16)
                link(nc.vector.tensor_tensor(bias_qv0[:, :], ps[:, 5, :], bias_qv0_in, ALU.add))

            def rest_of_setup():
                dve.wait_ge(loaded["ident"], 16)
                nc.vector.tensor_copy(ident_bf[:, :], ident).then_inc(s_ident_bf, 1)
                dve.wait_ge(s_bias1_ps, 1)
                nc.vector.tensor_tensor(bias_col[:, 1:3, :], ps[:, 4, 32:32 + 2 * KT].rearrange("p (i f) -> p i f", f=KT),
                                        bias_col_in[:, 1:3, :], ALU.add)
                nc.vector.tensor_tensor(bias_v1[:, :], ps[:, 5, D:2 * D], bias_v1_in, ALU.add)
                nc.vector.tensor_tensor(emb[:, :, :, :], ps[:, 4, 0:2 * 4 * B].rearrange("p (i o b) -> p i o b", i=2, o=4),
                                             b_emb[:, :, :].unsqueeze(3).to_broadcast([P, 2, 4, B]), ALU.add
                                        ).then_inc(s_bias1_read, 1)
                link(gains(1, (w_q1, w_k1, w_v1)))
                dve.wait_ge(s_bias1_read, 1)
                link(nc.vector.tensor_scalar(emb_s1[:, :, :, :], emb[:, :, 0:KT, :], 1.0, 0.5, ALU.add, ALU.mult))
                nc.vector.tensor_tensor(film[:, :, 0, :, :], emb_s1[:, :, :, :],
                                        ln2_w[:, :, :].unsqueeze(3).to_broadcast([P, 2, KT, B]), ALU.mult)
                link(nc.vector.tensor_tensor(emb_t[:, :, :, :], emb_s1[:, :, :, :],
                                             ln2_b[:, :, :].unsqueeze(3).to_broadcast([P, 2, KT, B]), ALU.mult))
                for i in range(2):
                    last = nc.vector.scalar_tensor_tensor(film[:, i, 1, :, :], emb[:, i, KT:2 * KT, :], 0.5,
                                                          emb_t[:, i, :, :], ALU.mult, ALU.add)
                last.then_inc(s_setup, 1)
                dve.wait_ge(s_setup, 1)

            def token_stats(i, src, n):
                return nc.vector.bn_stats(stats[i % 2][:, n, :], src[:, n, :])

            def mean_and_variance(i, b):
                m = i % 2
                nc.vector.tensor_copy(spare[:, i:i + 1], stats[m][:, 0, 0:1])
                for n in range(NT):
                    last = nc.vector.bn_aggr(mean_var[m][:, n, :], stats[m][:, n, :])
                last.then_inc(stats_ready[i].sem, 1)

            def norm_stats(i, b, src, step):
                for n in range(NT):
                    last = token_stats(i, src, n)
                step(last)
                mean_and_variance(i, b)

            def norm_tile(i, b, src, n):
                m = i % 2
                if n == 0:
                    dve.wait_ge(stats_ready[i].sem, stats_ready[i].at(b, 1))
                    dve.wait_ge(rstd_ready[i].sem, rstd_ready[i].at(b, 1))
                nc.vector.tensor_scalar(xn[m][:, n, :], src[:, n, :], mean_var[m][:, n, 0:1], rstd[m][:, n:n + 1],
                                        ALU.subtract, ALU.mult).then_inc(xn_ready[i].sem, 1)

            def norm_apply(i, b, src):
                for n in range(NT):
                    norm_tile(i, b, src, n)

            def silu(layer, b, f):
                if f == 0:
                    dve.wait_ge(tanh_ready[layer].sem, tanh_ready[layer].at(b, 1))
                nc.vector.scalar_tensor_tensor(tanh_h[:, f, :], tanh_h[:, f, :], 1.0, half_h[:, f, :],
                                               ALU.add, ALU.mult).then_inc(silu_ready[layer].sem, 1)

            def residual(layer, b, j, bank):
                if j == 0:
                    dve.wait_ge(plus_ready[layer].sem, plus_ready[layer].at(b, 1))
                dve.wait_ge(out_ps[layer].sem, out_ps[layer].at(b, j + 1))
                tiles = x[:, bass.ds(b, 1), 2 * j:2 * j + 2, :].rearrange("p a n d -> p (a n) d")
                nc.vector.tensor_tensor(tiles, ps[:, bank, :].rearrange("p (n d) -> p n d", d=D), tiles,
                                        ALU.add).then_inc(x_ready[layer].sem, 1)

            def this_batch(dst, first, count, b):
                return nc.vector.tensor_copy(dst, by_batch[:, first:first + count, bass.ds(b, 1)].rearrange("p a b -> p (a b)"))

            class StageA:
                def __init__(self, b):
                    self.b, self.step = b, Chain(dve, dve_a, b)

                def stats(self):
                    norm_stats(0, self.b, tokens_of(self.b), self.step)

                def mask(self):
                    dve.wait_ge(mask0_loaded.sem, mask0_loaded.at(self.b, 16))
                    self.step(nc.vector.tensor_scalar(mask0_wide[:, :], mask0_wide[:, :], 1.0, MASKED, ALU.subtract, ALU.mult))

                def keys(self, f):
                    dve.wait_ge(k0_ps.sem, k0_ps.at(self.b, f + 1))
                    self.step(nc.vector.scalar_tensor_tensor(k_exp[:, f, :], ps[:, 2 + f, :], bias_col[:, 0, f:f + 1],
                                                             mask0_wide[:, :], ALU.add, ALU.add))
                    nc.vector.tensor_reduce(k_negmax[:, f:f + 1], k_exp[:, f, :], AX.X, ALU.max, negate=True
                                            ).then_inc(k_max_ready.sem, 1)
                    if f == KT - 1:
                        self.step(this_batch(mask_now[:, :], 8, NT, self.b))

                def take_qv(self, n):
                    dve.wait_ge(qv_ps.sem, qv_ps.at(self.b, n + 1))
                    nc.vector.tensor_tensor(qv[:, n, :], ps[:, n, :], bias_qv0[:, :], ALU.add).then_inc(qv_read.sem, 1)

                def centre(self, j):
                    dve.wait_ge(qv_read.sem, qv_read.at(self.b, 2 * j + 2))
                    two = slice(2 * j, 2 * j + 2)
                    q_in = qv[:, two, 0:D].rearrange("p n (h l) -> p n h l", l=DH0)
                    self.step(nc.vector.tensor_reduce(q_max[:, two, :], q_in, AX.X, ALU.max))
                    for n in range(2):
                        last = nc.vector.tensor_tensor(q_in[:, n], q_in[:, n],
                                                       q_max[:, 2 * j + n, :].unsqueeze(2).to_broadcast([P, H0, DH0]), ALU.subtract)
                    last.then_inc(q_cent_ready.sem, 1)
                    assert j == 0 or self.step.k == dve_a.per_batch

            class StageB:
                def __init__(self, b, bank, wide):
                    self.b, self.step, self.bank, self.wide = b, Chain(dve, dve_b, b), bank, wide

                def attention(self):
                    this_batch(film_now[:, :], 0, 2 * KT, self.b)
                    dve.wait_ge(k_exp_ready.sem, k_exp_ready.at(self.b, KT))
                    self.step(nc.vector.reciprocal(k_rec[:, :], k_sum[:, :]))
                    dve.wait_ge(att_ps.sem, att_ps.at(self.b, 1))
                    for f in range(KT):
                        last = nc.vector.scalar_tensor_tensor(att[:, f, :], ps[:, self.bank, f * P:(f + 1) * P], k_rec[:, f:f + 1],
                                                              block_diag, ALU.mult, ALU.mult)
                    last.then_inc(att_ready.sem, 1)

                def sums(self):
                    dve.wait_ge(q_exp_ready.sem, q_exp_ready.at(self.b, 2))
                    self.step(nc.vector.tensor_reduce(q_sum[:, :], q_exp.rearrange("p n (h l) -> p (n h) l", l=DH0), AX.X, ALU.add))
                    self.step(nc.vector.reciprocal(q_rec[:, :], q_sum[:, :]))

                def output(self):
                    dve.wait_ge(y_ps.sem, y_ps.at(self.b, 1))
                    self.step(nc.vector.tensor_tensor(y[:, :, :].rearrange("p n (h l) -> p (n h) l", l=DH0),
                                                      ps[:, self.wide:self.wide + 2, :].rearrange("p n (h l) -> p (n h) l", l=DH0),
                                                      q_rec[:, :].unsqueeze(2).to_broadcast([P, NT * H0, DH0]), ALU.mult))
                    norm_stats(1, self.b, y, self.step)
                    assert self.step.k == dve_b.per_batch

                def silu(self):
                    for f in range(KT):
                        silu(0, self.b, f)

                def residual(self):
                    for j in range(2):
                        residual(0, self.b, j, self.wide + j)

            def stage_a(b):
                weights0()
                st = StageA(b)
                dve.wait_ge(loaded["x_first"], 16)
                st.stats()
                norm_apply(0, b, tokens_of(b))
                biases0()
                st.mask()
                for f in range(KT):
                    if f == KT - 1:
                        dve.wait_ge(loaded["masks"], 2 * 16)
                    st.keys(f)
                for j in range(2):
                    st.take_qv(2 * j)
                    st.take_qv(2 * j + 1)
                    st.centre(j)
                rest_of_setup()
                dve.wait_ge(loaded["x_rest"], 16)

            def both(b, early=False):
                new, old = StageA(b + 1), StageB(b, 4, 6)
                new.stats()
                old.attention()
                norm_apply(0, b + 1, tokens_of(b + 1))
                old.sums()
                new.mask()
                if early:
                    norm_stats(2, 0, tokens_of(0), Chain(dve, dve_pre, 0))
                old.output()
                new.keys(0)
                new.keys(1)
                if early:
                    norm_apply(2, 0, tokens_of(0))
                norm_apply(1, b, y)
                new.take_qv(0)
                new.take_qv(1)
                new.centre(0)
                old.silu()
                new.take_qv(2)
                new.take_qv(3)
                new.centre(1)
                old.residual()

            layer0(dve, stage_a, both)
            last_stage = StageB(B - 1, 0, OUTPUT)

            def last_b(s):
                if s == ATT_AT:
                    last_stage.attention()
                if s == Y_AT:
                    last_stage.sums()
                    last_stage.output()
                if s == NORM_AT:
                    norm_apply(1, B - 1, y)
                if s == SILU_AT:
                    last_stage.silu()
                if s == LAST_AT:
                    last_stage.residual()

            def maximum(b, g, m, n):
                i = (g * HG + m) * NT + n
                dve.wait_ge(a_ps.sem, a_ps.at(b, i + 1))
                nc.vector.tensor_reduce(row_max[:, g, n, m:m + 1], ps[:, MAXIMA + i % 2, :], AX.X, ALU.max
                                        ).then_inc(a_read.sem, 1)

            def split_max(b, g):
                step = Chain(dve, dve_att, b)
                step.k = 2 * g
                dve.wait_ge(a_read.sem, a_read.at(b, (g + 1) * HG * NT))
                step(nc.vector.tensor_scalar(max_part[:, g, :, 0, :], row_max[:, g, :, :], -1.0, None, ALU.mult))
                step(nc.vector.tensor_tensor(max_rest[:, g, :, :], row_max[:, g, :, :], max_part[:, g, :, 0, :], ALU.add))
                nc.vector.tensor_scalar(max_part[:, g, :, 1, :], max_rest[:, g, :, :], -1.0, None, ALU.mult
                                        ).then_inc(max_part_ready.sem, 1)

            def normalise(b, g):
                step = Chain(dve, norm_y, b)
                step.k = g
                dve.wait_ge(o_tp_ps.sem, o_tp_ps.at(b, g + 1))
                o = ps[:, TURNED, :].rearrange("p (n h c) -> p n h c", n=NT, h=HG)
                step(nc.vector.reciprocal(o_rec[:, g, :, :], o[:, :, :, DH1]))
                nc.vector.tensor_tensor(
                    y[:, :, g * HG * DH1:(g + 1) * HG * DH1].rearrange("p n (h l) -> p n h l", l=DH1),
                    o[:, :, :, 0:DH1], o_rec[:, g, :, :].unsqueeze(3).to_broadcast([P, NT, HG, DH1]), ALU.mult
                ).then_inc(y1_done.sem, 1)

            def take_v(b, j):
                dve.wait_ge(v_ps.sem, v_ps.at(b, j + 1))
                nc.vector.tensor_tensor(v_sum[:, 2 * j:2 * j + 2, :], ps[:, SIDE, :].rearrange("p (n d) -> p n d", d=D),
                                        bias_v1[:, :].unsqueeze(1).to_broadcast([P, 2, D]), ALU.add
                                        ).then_inc(v_sum_ready.sem, 1)
                if j == 1:
                    this_batch(mask_now[:, :], 12, NT, b).then_inc(mask_now_ready.sem, 1)

            def read_side(pre, post, s):
                if post is not None and s in OUT_AT:
                    residual(1, post, OUT_AT.index(s), SIDE)
                if pre is not None and piece(pre, s)[0] == "v":
                    take_v(pre, piece(pre, s)[1])

            def between(pre, att_b, post, s, n):
                if n == 0:
                    read_side(pre, post, s - 1)
                if pre is not None and not first(pre):
                    src = tokens_of(pre)
                    if s == 0:
                        last = token_stats(2, src, n)
                        if n == NT - 1:
                            Chain(dve, dve_pre, pre)(last)
                            mean_and_variance(2, pre)
                    if s == 1 and n >= 1:
                        for tile in ((), (0, 1), (2,), (3,))[n]:
                            norm_tile(2, pre, src, tile)
                if post is not None:
                    if s == 1 and n == 3:
                        normalise(post, G - 1)
                    if s == 3:
                        if n == 0:
                            dve.wait_ge(y1_done.sem, y1_done.at(post, G))
                        last = token_stats(3, y, n)
                        if n == NT - 1:
                            step = Chain(dve, dve_post, post)
                            step(last)
                            mean_and_variance(3, post)
                            step(this_batch(film_now[:, :], 2 * KT, 2 * KT, post))
                    if s == 4:
                        norm_tile(3, post, y, n)
                    if s == OUT_AT[0] - 1 and n in (1, 3):
                        silu(1, post, n // 2)
                if att_b is not None:
                    if s in (5, 9, 13) and n == 1:
                        normalise(att_b, s // NT - 1)

            def turn(pre, att_b, post, beside=lambda s: None):
                for s in range(STEPS):
                    beside(s)
                    b, g, m = maxima_at(pre, att_b, s)
                    for n in range(NT):
                        if b is not None:
                            maximum(b, g, m, n)
                        between(pre, att_b, post, s, n)
                    if b is not None and m == HG - 1:
                        split_max(b, g)

            def last_post():
                b = B - 1
                normalise(b, G - 1)
                dve.wait_ge(y1_done.sem, y1_done.at(b, G))
                this_batch(film_now[:, :], 2 * KT, 2 * KT, b)
                for j in range(2):
                    for n in (2 * j, 2 * j + 1):
                        last = token_stats(3, y, n)
                    last.then_inc(tail["sum"], 1)
                    dve.wait_ge(tail["sum"], j + 1)
                    for n in (2 * j, 2 * j + 1):
                        last = nc.vector.bn_aggr(mean_var[1][:, n, :], stats[1][:, n, :])
                    last.then_inc(tail["stats"], 1)
                for j in range(2):
                    dve.wait_ge(tail["stats"], j + 1)
                    dve.wait_ge(tail["rstd"], j + 1)
                    for n in (2 * j, 2 * j + 1):
                        nc.vector.tensor_scalar(xn[1][:, n, :], y[:, n, :], mean_var[1][:, n, 0:1], rstd[1][:, n:n + 1],
                                                ALU.subtract, ALU.mult).then_inc(tail["xn"], 1)
                for j in range(2):
                    dve.wait_ge(tail["tanh"], j + 1)
                    nc.vector.scalar_tensor_tensor(tanh_h[:, :, half_of(j)], tanh_h[:, :, half_of(j)], 1.0,
                                                   half_h[:, :, half_of(j)], ALU.add, ALU.mult).then_inc(tail["silu"], 1)
                dve.wait_ge(plus_ready[1].sem, plus_ready[1].at(b, 1))
                for j in range(2):
                    dve.wait_ge(tail["out"], j + 1)
                    tiles = x[:, b, 2 * j:2 * j + 2, :]
                    nc.vector.tensor_tensor(tiles, ps[:, OUT_BANKS[j], :].rearrange("p (n d) -> p n d", d=D), tiles,
                                            ALU.add).then_inc(tail["x"], 1)

            layer1(dve, turn, last_b, last_post)

        @block.tensor
        def _(pe):
            mm = nc.tensor.matmul
            def keep_warm(count, bank):
                for _ in range(count):
                    mm(ps[:, bank, :], zeros[:, 0:P], zeros[:, :], start=True, stop=True)

            pe.wait_ge(s_zeros, 1)
            keep_warm(WARM_START, 7)
            def bias_column(to, wt, layer):
                for o in range(KT):
                    for f in range(KT):
                        last = mm(to[:, o:o + 1], wt[:, f, o * P:(o + 1) * P], ln_b[:, layer, f:f + 1],
                                  start=(f == 0), stop=(f == KT - 1))
                return last

            def bias_row(to, wt, layer):
                for f in range(KT):
                    last = mm(to, ln_b_wide[:, layer, f, :], wt[:, f, :], start=(f == 0), stop=(f == KT - 1))
                return last

            def rest_of_setup():
                pe.wait_ge(qv_read.sem, 1)
                pe.wait_ge(loaded["w_emb"], 2 * 16)
                pe.wait_ge(s_cond_t, 1)
                for i in range(2):
                    for c in range(TE // P):
                        last = mm(ps[32 * c:32 * c + 32, 6 + i, :], cond_t[:, c, :], w_emb[i][:, c, :], start=True, stop=True)
                    last.then_inc(s_part_ps, 1)
                pe.wait_ge(loaded["w_qkv1"], 3 * 16)
                bias_row(ps[:, 5, D:2 * D], w_v1, 1)
                for side, wt in enumerate((w_q1, w_k1)):
                    for f in range(KT):
                        c = KT * side + f
                        last = mm(ps[32 * c:32 * c + 32, 5, 0:D], ln_b_wide[:, 1, f, 0:32], wt[:, f, :], start=True, stop=True)
                last.then_inc(s_part_ps, 1)
                keep_warm(WARM_PARTS, 4)
                for i in range(2):
                    pe.wait_ge(s_part, i + 1)
                    for o in range(4):
                        q = (i * 4 + o) * B
                        mm(ps[:, 4, q:q + B], cond_part[:, i, o * P:(o + 1) * P], sum_batches, start=True, stop=True)
                pe.wait_ge(s_part, 3)
                for o in range(KT):
                    last = mm(ps[:, 4, 32 + o:32 + 2 * KT:KT], bias_part[:, o * P:(o + 1) * P], sum_sides, start=True, stop=True)
                last.then_inc(s_bias1_ps, 1)
                pe.wait_ge(loaded["w_out"], 2 * 16)
                pe.wait_ge(s_bias1_read, 1)

            pe.wait_ge(loaded["cols"], 16)
            pe.wait_ge(s_wide, 1)
            pe.wait_ge(loaded["w_k0_qv0"], 3 * 16)
            bias_column(ps[:, 4, 0:KT], w_k0, 0)
            bias_row(ps[:, 5, :], w_qv0, 0).then_inc(s_bias0_ps, 1)
            pe.wait_ge(loaded["ident"], 16)

            def turn_xn(i, b, f, bank):
                for n in range(NT):
                    if f == 0:
                        pe.wait_ge(xn_ready[i].sem, xn_ready[i].at(b, n + 1))
                    last = nc.tensor.transpose(ps[:, bank, n * P:(n + 1) * P], xn[i % 2][:, n, f * P:(f + 1) * P], ident)
                last.then_inc(tp_ready[i].sem, 1)

            def turn_half(i, b, f, bank, half):
                for n in (2 * half, 2 * half + 1):
                    if f == 0:
                        pe.wait_ge(xn_ready[i].sem, xn_ready[i].at(b, n + 1))
                    last = nc.tensor.transpose(ps[:, bank, n * P:(n + 1) * P], xn[i % 2][:, n, f * P:(f + 1) * P], ident)
                if half == 1:
                    last.then_inc(tp_ready[i].sem, 1)

            def qk_half(k, bank, half):
                wt, o = (w_q1, w_k1)[k % 2], k // 2
                last = mm(ps[:, bank, :], wt[:, half, o * P:(o + 1) * P], xn_t[1][:, half, :],
                          start=(half == 0), stop=(half == KT - 1))
                if half == 1:
                    last.then_inc(qk_ps.sem, 1)

            def features(bank, wt, o):
                for f in range(KT):
                    last = mm(ps[:, bank, :], wt[:, f, o * P:(o + 1) * P], xn_t[0][:, f, :], start=(f == 0), stop=(f == KT - 1))
                return last

            def tokens(out_cols, left, wt, n, width):
                for f in range(KT):
                    last = mm(out_cols, left[:, f, n * P:(n + 1) * P], wt[:, f, 0:width], start=(f == 0), stop=(f == KT - 1))
                return last

            def project_out(layer, b, j, bank):
                pe.wait_ge(silu_ready[layer].sem, silu_ready[layer].at(b, KT))
                for n in (2 * j, 2 * j + 1):
                    last = tokens(ps[:, bank, (n % 2) * D:(n % 2 + 1) * D], tanh_h, w_out[layer], n, D)
                last.then_inc(out_ps[layer].sem, 1)

            def a_turn(b):
                for f in range(KT):
                    turn_xn(0, b, f, f)

            def a_keys(b):
                pe.wait_ge(xnt_ready[0].sem, xnt_ready[0].at(b, KT))
                for o in range(KT):
                    features(2 + o, w_k0, o).then_inc(k0_ps.sem, 1)

            def a_qv(b, tiles):
                for n in tiles:
                    if n >= 2:
                        pe.wait_ge(k_max_ready.sem, k_max_ready.at(b, n - 1))
                    tokens(ps[:, n, :], xn_t[0], w_qv0, n, 2 * D).then_inc(qv_ps.sem, 1)

            def b_turn(b, bank, q_bank):
                pe.wait_ge(k_exp_ready.sem, k_exp_ready.at(b, KT))
                pe.wait_ge(q_exp_ready.sem, q_exp_ready.at(b, 1))
                for n in range(NT):
                    for f in range(KT):
                        c = (n % 2) * D + f * P
                        last = nc.tensor.transpose(ps[:, bank + n // 2, c:c + P], k_exp[:, f, n * P:(n + 1) * P], ident)
                last.then_inc(k_tok_ps.sem, 1)
                pe.wait_ge(q_exp_ready.sem, q_exp_ready.at(b, 2))
                for n in range(NT):
                    for f in range(KT):
                        last = nc.tensor.transpose(ps[:, q_bank + f, n * P:(n + 1) * P], q_exp[:, n, f * P:(f + 1) * P], ident)
                last.then_inc(q_t_ps.sem, 1)

            def b_attention(b, bank):
                pe.wait_ge(k_tok_ready.sem, k_tok_ready.at(b, 1))
                pe.wait_ge(v0_ready.sem, v0_ready.at(b, NT))
                for f in range(KT):
                    for n in range(NT):
                        last = mm(ps[:, bank, f * P:(f + 1) * P], k_tok[:, n, f * P:(f + 1) * P],
                                  qv[:, n, D + f * P:D + (f + 1) * P], start=(n == 0), stop=(n == NT - 1))
                last.then_inc(att_ps.sem, 1)

            def b_output(b, wide):
                pe.wait_ge(att_ready.sem, att_ready.at(b, 1))
                pe.wait_ge(q_t_ready.sem, q_t_ready.at(b, 1))
                for n in range(NT):
                    for f in range(KT):
                        c = (n % 2) * D + f * P
                        last = mm(ps[:, wide + n // 2, c:c + P], q_t[:, f, n * P:(n + 1) * P], att[:, f, :], start=True, stop=True)
                last.then_inc(y_ps.sem, 1)

            def b_turn_xn(b, banks):
                for f in range(KT):
                    turn_xn(1, b, f, banks[f])

            def b_project(b, wide):
                for j in range(2):
                    project_out(0, b, j, wide + j)

            def stage_a(b):
                a_turn(b)
                keep_warm(WARM_NORM, 7)
                pe.wait_ge(s_weights0, 1)
                a_keys(b)
                a_qv(b, range(NT))
                rest_of_setup()

            def both(b, early=False):
                b_turn(b, 4, 2)
                b_attention(b, 4)
                a_turn(b + 1)
                b_output(b, 6)
                a_keys(b + 1)
                a_qv(b + 1, (0, 1))
                if early:
                    keep_warm(WARM_EARLY, EARLY_BANK)
                    turn_xn(2, 0, 0, EARLY_BANK)
                b_turn_xn(b, (4, 6) if early else (4, 5))
                if early:
                    pe.wait_ge(xnt_ready[1].sem, xnt_ready[1].at(0, 1))
                    turn_xn(2, 0, 1, EARLY_BANK)
                a_qv(b + 1, (2,))
                if early:
                    pe.wait_ge(xnt_ready[1].sem, xnt_ready[1].at(0, 2))
                    qk_half(0, EARLY_BANK, 0)
                    qk_half(0, EARLY_BANK, 1)
                a_qv(b + 1, (3,))
                if early:
                    pe.wait_ge(qk_ready.sem, qk_ready.at(0, 1))
                    qk_half(1, EARLY_BANK, 0)
                    qk_half(1, EARLY_BANK, 1)
                b_project(b, 6)

            layer0(pe, stage_a, both)
            pe.wait_ge(s_ident_bf, 1)
            pe.wait_ge(s_setup, 1)
            pe.wait_ge(s_setup_pool, SETUP_POOL)

            def last_b(s):
                if s == TURN_AT:
                    b_turn(B - 1, 0, 2)
                if s == ATT_AT:
                    b_attention(B - 1, 0)
                if s == Y_AT:
                    b_output(B - 1, OUTPUT)
                if s == XN_AT:
                    b_turn_xn(B - 1, (0, 1))
                if s == LAST_AT:
                    b_project(B - 1, OUTPUT)

            def maximum(b, g, m, n):
                h = g * HG + m
                if m == 0 and n == 0:
                    pe.wait_ge(stack_loaded[g].sem, stack_loaded[g].at(b, 3 * 16))
                i = h * NT + n
                if i >= 2:
                    pe.wait_ge(a_read.sem, a_read.at(b, i - 1))
                elif not first(b):
                    pe.wait_ge(a_read.sem, a_read.at(b - 1, STEPS * HG + i - 1))
                mm(ps[:, MAXIMA + i % 2, :], q_stack[0:K_MAX, h, n * P:(n + 1) * P], k_stack[0:K_MAX, h, :],
                   start=True, stop=True).then_inc(a_ps.sem, 1)

            def turn_max(b, g):
                pe.wait_ge(max_part_ready.sem, max_part_ready.at(b, g + 1))
                if g >= 2:
                    pe.wait_ge(y1_done.sem, y1_done.at(b, g - 1))
                elif not first(b):
                    pe.wait_ge(y1_done.sem, y1_done.at(b - 1, G - 1 + g))
                elif g == 1:
                    pe.wait_ge(max_row_ready.sem, max_row_ready.at(b, 1))
                for n in range(NT):
                    last = nc.tensor.transpose(ps[0:2 * HG, TURNED, n * P // 2:(n + 1) * P // 2].bitcast(BF16),
                                               max_part[:, g, n, :, :].rearrange("p a h -> p (a h)"), ident_bf[:, :])
                last.then_inc(max_row_ps.sem, 1)

            def scores(b, s, hh):
                g, m = divmod(s, NT)
                if m == 0 and hh == 0:
                    pe.wait_ge(max_loaded[g].sem, max_loaded[g].at(b, 32))
                u = HG * s + hh
                if u >= 3:
                    pe.wait_ge(probs_ready.sem, probs_ready.at(b, u - 2))
                elif not first(b):
                    last_in_bank = max(v for v in range(STEPS * HG) if v % 3 == u)
                    pe.wait_ge(probs_ready.sem, probs_ready.at(b - 1, last_in_bank + 1))
                mm(ps[:, SCORES + u % 3, :], k_stack[0:K_EXP, g * HG + hh, m * P:(m + 1) * P], q_stack[0:K_EXP, g * HG + hh, :],
                   start=True, stop=True).then_inc(s_ps.sem, 1)

            def weigh(b, s):
                g, m = divmod(s, NT)
                if g == 0:
                    pe.wait_ge(v1_ready.sem, v1_ready.at(b, m + 1))
                if m == 0:
                    if g >= 1:
                        pe.wait_ge(o_copied.sem, o_copied.at(b, g))
                    elif not first(b):
                        pe.wait_ge(o_copied.sem, o_copied.at(b - 1, G))
                for hh in range(HG):
                    pe.wait_ge(probs_ready.sem, probs_ready.at(b, HG * s + hh + 1))
                    last = mm(ps[32 * hh:32 * hh + 32, OUTPUT, :], v1[:, m, g * HG + hh, :], probs[:, s % PROBS, hh, :],
                              start=(m == 0), stop=(m == NT - 1))
                last.then_inc(probs_used.sem, 1)

            def turn_o(b, g):
                pe.wait_ge(o_copied.sem, o_copied.at(b, g + 1))
                if g < G - 1:
                    pe.wait_ge(max_row_ready.sem, max_row_ready.at(b, g + 2))
                elif isinstance(b, int) and b == B - 1:
                    pe.wait_ge(y1_done.sem, y1_done.at(b, G - 1))
                else:
                    pe.wait_ge(max_row_ready.sem, max_row_ready.at(b + 1, 1))
                for n in range(NT):
                    last = nc.tensor.transpose(ps[:, TURNED, n * P:(n + 1) * P], o_sb[:, g % 2, n * P:(n + 1) * P], ident)
                last.then_inc(o_tp_ps.sem, 1)

            def side(pre, post, s, half):
                if pre is not None:
                    what, k = piece(pre, s)
                    if what == "xn":
                        if half == 0 and k == 1:
                            pe.wait_ge(xnt_ready[1].sem, xnt_ready[1].at(pre, 1))
                        if half == 0 and k == 0:
                            pe.wait_ge(v_sum_ready.sem, v_sum_ready.at(pre - 1, 2))
                        turn_half(2, pre, k, SIDE, half)
                    if what == "qk":
                        if half == 0:
                            if k == 0:
                                pe.wait_ge(xnt_ready[1].sem, xnt_ready[1].at(pre, 2))
                            else:
                                pe.wait_ge(qk_ready.sem, qk_ready.at(pre, k))
                            if k == 2 and post is not None:
                                pe.wait_ge(half_ready[1].sem, half_ready[1].at(post, 2))
                            if k == 2 and first(pre):
                                pe.wait_ge(x_ready[0].sem, x_ready[0].at(B - 2, 2))
                        qk_half(k, SIDE, half)
                    if what == "v":
                        if half == 0 and k == 0:
                            pe.wait_ge(qk_ready.sem, qk_ready.at(pre, 4))
                            if post is not None:
                                pe.wait_ge(x_ready[1].sem, x_ready[1].at(post, 2))
                        if half == 0 and k == 1:
                            pe.wait_ge(v_sum_ready.sem, v_sum_ready.at(pre, 1))
                        last = tokens(ps[:, SIDE, half * D:(half + 1) * D], xn_t[1], w_v1, 2 * k + half, D)
                        if half == 1:
                            last.then_inc(v_ps.sem, 1)
                if post is not None:
                    if s in XN_POST:
                        f = XN_POST.index(s)
                        if half == 0 and f == 1:
                            pe.wait_ge(half_ready[1].sem, half_ready[1].at(post, 1))
                        if half == 0 and f == 0 and pre is not None:
                            pe.wait_ge(qk_ready.sem, qk_ready.at(pre, 2))
                        turn_half(3, post, f, SIDE, half)
                    if s in OUT_AT:
                        j = OUT_AT.index(s)
                        if half == 0 and j == 0:
                            pe.wait_ge(silu_ready[1].sem, silu_ready[1].at(post, KT))
                            if pre is not None:
                                pe.wait_ge(qk_ready.sem, qk_ready.at(pre, 4))
                        if half == 0 and j == 1:
                            pe.wait_ge(x_ready[1].sem, x_ready[1].at(post, 1))
                        last = tokens(ps[:, SIDE, half * D:(half + 1) * D], tanh_h, w_out[1], 2 * j + half, D)
                        if half == 1:
                            last.then_inc(out_ps[1].sem, 1)

            def turn(pre, att_b, post, beside=lambda s: None):
                for s in range(STEPS):
                    beside(s)
                    b, g, m = maxima_at(pre, att_b, s)
                    for hh in range(HG):
                        if att_b is not None:
                            scores(att_b, s, hh)
                        if b is not None:
                            maximum(b, g, m, hh)
                            if att_b is None:
                                keep_warm(1, 2)
                            elif first(att_b) and s < 2:
                                keep_warm(1, TURNED)
                        if hh == 0:
                            side(pre, post, s - 1, 1)
                            if att_b is not None and s in (5, 9, 13):
                                turn_o(att_b, s // NT - 1)
                            if post is not None and s == 1:
                                turn_o(post, G - 1)
                        if hh == 1:
                            if att_b is not None and s >= 1:
                                weigh(att_b, s - 1)
                            if post is not None and s == 0:
                                weigh(post, STEPS - 1)
                        if hh == 1:
                            row_b, row_g = rows_turned_at(pre, att_b, s)
                            if row_b is not None:
                                turn_max(row_b, row_g)
                        if hh == 2:
                            side(pre, post, s, 0)

            def last_post():
                b = B - 1
                weigh(b, STEPS - 1)
                turn_o(b, G - 1)
                keep_warm(WARM_LAST_NORM, OUTPUT)
                for j in range(2):
                    for f in range(KT):
                        for n in (2 * j, 2 * j + 1):
                            pe.wait_ge(tail["xn"], n + 1)
                            last = nc.tensor.transpose(ps[:, KT * j + f, (n % 2) * P:(n % 2 + 1) * P],
                                                       xn[1][:, n, f * P:(f + 1) * P], ident)
                        last.then_inc(tail["tp"], 1)
                keep_warm(WARM_LAST_TANH, OUTPUT)
                for j in range(2):
                    pe.wait_ge(tail["silu"], j + 1)
                    for n in (2 * j, 2 * j + 1):
                        last = tokens(ps[:, OUT_BANKS[j], (n % 2) * D:(n % 2 + 1) * D], tanh_h, w_out[1], n, D)
                    last.then_inc(tail["out"], 1)

            layer1(pe, turn, last_b, last_post)


_INS = ['x', 'mask_BxSx1_fk1', 'mask_BxS_ff1', 'L0_cond_Wq', 'L0_cond_Wk', 'L0_cond_Wv', 'L0_cond_W_emb', 'L0_cond_W_out',
        'L1_cond_q_w', 'L1_cond_k_w', 'L1_cond_v_w', 'L1_cond_emb_w', 'L1_cond_out_w']


def kernel(**inputs):
    import numpy as np
    import concourse.bacc as bacc
    from concourse.bass_utils import run_bass_kernel_spmd

    nc = bacc.Bacc("TRN2", target_bir_lowering=False, num_devices=1)
    arrays = {name: np.ascontiguousarray(inputs[name]) for name in _INS}
    by_feature = lambda v: v.reshape(*v.shape[:-1], KT, P // DH1, DH1).swapaxes(-1, -2).reshape(v.shape)
    for name in ("L1_cond_q_w", "L1_cond_k_w"):
        arrays[name] = np.ascontiguousarray(by_feature(inputs[name]))
    column = lambda *names: [inputs[n].reshape(-1, P).T for n in names]
    pairs = (("ln_w", "norm_w"), ("ln_b", "norm_b"), ("ln2_w", "sb_norm_w"), ("ln2_b", "sb_norm_b"), ("b_emb", "emb_b"))
    arrays["cols"] = np.ascontiguousarray(np.concatenate(
        [c for p0, p1 in pairs for c in column("L0_cond_" + p0, "L1_cond_" + p1)]
        + column("L0_cond_bk") + [by_feature(inputs[n]).reshape(-1, P).T for n in ("L1_cond_q_b", "L1_cond_k_b")]
        + [inputs["cond_2048"].reshape(B, TE // P, P).transpose(2, 1, 0).reshape(P, -1)], axis=1))
    arrays["mask_cols"] = np.ascontiguousarray(np.concatenate(
        [inputs[n].reshape(B, NT, P).transpose(2, 1, 0) for n in ("mask_BxSx1_fk1", "mask_BxS_ff1")], axis=1))
    arrays["vectors"] = np.concatenate([inputs[n] for n in (
        "L0_cond_bq", "L0_cond_bv", "L1_cond_v_b", "L0_cond_b_out", "L1_cond_out_b")])
    row = np.arange(P)
    arrays["consts"] = np.concatenate([
        row[:, None] == row, row[:, None] // DH0 == row // DH0, row[:, None] % 32 == np.arange(B),
        (row[:, None] % 32 == 0) & (row[:, None] // 32 // KT == np.arange(2))], axis=1).astype(np.float32)
    aps = {name: nc.dram_tensor(f"in_{name}", v.shape, mybir.dt.from_np(v.dtype), kind="ExternalInput").ap()
           for name, v in arrays.items()}
    out = nc.dram_tensor("out_0", (B, T, D), F32, kind="ExternalOutput").ap()
    build(nc, aps, out)
    r = run_bass_kernel_spmd(nc, [{f"in_{name}": v for name, v in arrays.items()}], core_ids=[0])
    return r.results[0]["out_0"]
```
